# Optimizing a Trainium2 kernel written in Bass

```python
import numpy as np
import jax
import jax.numpy as jnp

def _softmax(x, axis=-1):
    return jax.nn.softmax(x, axis=axis)

def _gelu(x):
    return jax.nn.gelu(x, approximate=True)

def _silu(x):
    return jax.nn.silu(x)

def _sigmoid(x):
    return jax.nn.sigmoid(x)

def _layernorm(x, axis=-1, eps=1e-05):
    m = jnp.mean(x, axis=axis, keepdims=True)
    v = jnp.var(x, axis=axis, keepdims=True)
    return (x - m) / jnp.sqrt(v + eps)

def _scatter_add(tgt, idx, src, axis=0):
    return tgt.at[idx].add(src)

def _segment_sum(src, seg, n):
    return jax.ops.segment_sum(src, seg, n)
kernel_name = 'mk_audio_tower_d1_tok_audfeat256_r4_579793'

def setup_inputs(seed: int=0):
    np.random.seed(seed)
    _w = jnp.asarray

    def _rec_inputs():
        import jax
        import jax.numpy as jnp
        _rk = jax.random.key(seed)
        x = -5.07413e-05 + 0.999912 * jax.random.normal(jax.random.fold_in(_rk, 1), (64, 125, 64), jnp.float32)
        return x
    x = _rec_inputs()

    def _L0_tok_setup():
        import jax, jax.numpy as jnp
        from jax import lax
        import numpy as np
        B, T, C, K, STRIDE = (16, 4000, 64, 5, 2)
        EPS = 0.001
        key = jax.random.key(seed)
        k0, k1, k2, k3 = jax.random.split(key, 4)
        x = jax.random.normal(k0, (B, T, C), dtype=jnp.float32)
        w = jax.random.normal(k1, (K, 1, C), dtype=jnp.float32) * 0.1
        b = jax.random.normal(k2, (C,), dtype=jnp.float32) * 0.01
        gamma = jnp.ones((C,), dtype=jnp.float32)
        beta = jnp.zeros((C,), dtype=jnp.float32)
        alpha = jnp.full((C,), 0.25, dtype=jnp.float32) + 0.01 * jax.random.normal(k3, (C,), dtype=jnp.float32)
        return {'x': x, 'w': w, 'b': b, 'gamma': gamma, 'beta': beta, 'alpha': alpha}
    _L0_tok_all = _L0_tok_setup()
    _L0_tok_in = {k: v for k, v in _L0_tok_all.items() if k in ('w', 'b', 'gamma', 'beta', 'alpha')}
    del _L0_tok_all

    def _L0_attn_setup():
        import jax, jax.numpy as jnp
        import numpy as np
        import math
        B, T, D_MODEL = (1, 512, 64)
        N_Q, N_KV = (16, 1)
        D_HEAD = D_MODEL // N_KV
        QPG = N_Q // N_KV
        ROPE_BASE = 10000.0
        WINDOW = 128
        EPS = 1.1920929e-07
        NEG = -1e+30

        def _rope(x, base=ROPE_BASE):
            t, d = (x.shape[-2], x.shape[-1])
            freqs = base ** (-2.0 * jnp.arange(d // 2, dtype=jnp.float32) / d)
            theta = jnp.arange(t, dtype=jnp.float32)[:, None] * freqs[None, :]
            cos, sin = (jnp.cos(theta), jnp.sin(theta))
            x1, x2 = (x[..., 0::2], x[..., 1::2])
            r1 = x1 * cos - x2 * sin
            r2 = x1 * sin + x2 * cos
            return jnp.stack([r1, r2], axis=-1).reshape(x.shape)

        def _rmsnorm(x, w):
            return x * jax.lax.rsqrt(jnp.mean(x * x, axis=-1, keepdims=True) + EPS) * w
        key = jax.random.key(seed)
        k0, k1, k2, k3 = jax.random.split(key, 4)
        x = jax.random.normal(k0, (B, T, D_MODEL), dtype=jnp.float32)
        wq = jax.random.normal(k1, (QPG * N_KV * D_HEAD, D_MODEL), dtype=jnp.float32) * 0.02
        wkv = jax.random.normal(k2, (2 * D_HEAD * N_KV, D_MODEL), dtype=jnp.float32) * 0.02
        wo = jax.random.normal(k3, (D_MODEL, D_HEAD * N_Q * N_KV), dtype=jnp.float32) * 0.02
        q_norm_w = jnp.ones((D_HEAD,), dtype=jnp.float32)
        k_norm_w = jnp.ones((D_HEAD,), dtype=jnp.float32)
        return {'x': x, 'wq': wq, 'wkv': wkv, 'wo': wo, 'q_norm_w': q_norm_w, 'k_norm_w': k_norm_w}
    _L0_attn_all = _L0_attn_setup()
    _L0_attn_in = {k: v for k, v in _L0_attn_all.items() if k in ('wq', 'wkv', 'wo', 'q_norm_w', 'k_norm_w')}
    del _L0_attn_all

    def _L0_ffn_setup():
        import jax, jax.numpy as jnp
        import numpy as np
        B, T, IN_DIM = (64, 64, 64)
        HID, OUT_DIM = (128, 64)
        N_LAYERS, N_EXPERTS, N_SHARED = (2, 16, 1)
        key = jax.random.key(seed)
        ks = jax.random.split(key, 10)
        s = 0.02
        x = jax.random.normal(ks[0], (B, T, IN_DIM), dtype=jnp.float32)
        route_id = jax.random.randint(ks[1], (B,), 0, N_EXPERTS)
        Wi = jax.random.normal(ks[2], (HID, IN_DIM), dtype=jnp.float32) * s
        bi = jnp.zeros((HID,), dtype=jnp.float32)
        Wr = jax.random.normal(ks[3], (N_LAYERS, N_EXPERTS, HID, HID), dtype=jnp.float32) * s
        br = jax.random.normal(ks[4], (N_LAYERS, N_EXPERTS, HID), dtype=jnp.float32) * s
        Ws = jax.random.normal(ks[5], (N_LAYERS, N_SHARED, HID, HID), dtype=jnp.float32) * s
        bs = jax.random.normal(ks[6], (N_LAYERS, N_SHARED, HID), dtype=jnp.float32) * s
        Wo = jax.random.normal(ks[7], (OUT_DIM, HID), dtype=jnp.float32) * s
        bo = jnp.zeros((OUT_DIM,), dtype=jnp.float32)
        return {'x': x, 'route_id': route_id, 'Wi': Wi, 'bi': bi, 'Wr': Wr, 'br': br, 'Ws': Ws, 'bs': bs, 'Wo': Wo, 'bo': bo}
    _L0_ffn_all = _L0_ffn_setup()
    _L0_ffn_in = {k: v for k, v in _L0_ffn_all.items() if k in ('route_id', 'Wi', 'bi', 'Wr', 'br', 'Ws', 'bs', 'Wo', 'bo')}
    del _L0_ffn_all
    return {'x': x, 'L0_tok_w': _L0_tok_in['w'], 'L0_tok_b': _L0_tok_in['b'], 'L0_tok_gamma': _L0_tok_in['gamma'], 'L0_tok_beta': _L0_tok_in['beta'], 'L0_tok_alpha': _L0_tok_in['alpha'], 'L0_attn_wq': _L0_attn_in['wq'], 'L0_attn_wkv': _L0_attn_in['wkv'], 'L0_attn_wo': _L0_attn_in['wo'], 'L0_attn_q_norm_w': _L0_attn_in['q_norm_w'], 'L0_attn_k_norm_w': _L0_attn_in['k_norm_w'], 'L0_ffn_route_id': _L0_ffn_in['route_id'], 'L0_ffn_Wi': _L0_ffn_in['Wi'], 'L0_ffn_bi': _L0_ffn_in['bi'], 'L0_ffn_Wr': _L0_ffn_in['Wr'], 'L0_ffn_br': _L0_ffn_in['br'], 'L0_ffn_Ws': _L0_ffn_in['Ws'], 'L0_ffn_bs': _L0_ffn_in['bs'], 'L0_ffn_Wo': _L0_ffn_in['Wo'], 'L0_ffn_bo': _L0_ffn_in['bo']}

def reference(x, L0_tok_w, L0_tok_b, L0_tok_gamma, L0_tok_beta, L0_tok_alpha, L0_attn_wq, L0_attn_wkv, L0_attn_wo, L0_attn_q_norm_w, L0_attn_k_norm_w, L0_ffn_route_id, L0_ffn_Wi, L0_ffn_bi, L0_ffn_Wr, L0_ffn_br, L0_ffn_Ws, L0_ffn_bs, L0_ffn_Wo, L0_ffn_bo):
    import jax
    import jax.numpy as jnp

    def _L0_tok_ref(x, w, b, gamma, beta, alpha):
        import jax, jax.numpy as jnp
        from jax import lax
        import numpy as np
        B, T, C, K, STRIDE = (16, 4000, 64, 5, 2)
        EPS = 0.001
        y = lax.conv_general_dilated(x, w, window_strides=(STRIDE,), padding='SAME', dimension_numbers=('NWC', 'WIO', 'NWC'), feature_group_count=C) + b
        mean = jnp.mean(y, axis=(1, 2), keepdims=True)
        var = jnp.var(y, axis=(1, 2), keepdims=True)
        yn = (y - mean) * lax.rsqrt(var + EPS) * gamma + beta
        return jnp.where(yn > 0, yn, alpha * yn)

    def _L0_attn_ref(x, wq, wkv, wo, q_norm_w, k_norm_w):
        import jax, jax.numpy as jnp
        import numpy as np
        import math
        B, T, D_MODEL = (1, 512, 64)
        N_Q, N_KV = (16, 1)
        D_HEAD = D_MODEL // N_KV
        QPG = N_Q // N_KV
        ROPE_BASE = 10000.0
        WINDOW = 128
        EPS = 1.1920929e-07
        NEG = -1e+30

        def _rope(x, base=ROPE_BASE):
            t, d = (x.shape[-2], x.shape[-1])
            freqs = base ** (-2.0 * jnp.arange(d // 2, dtype=jnp.float32) / d)
            theta = jnp.arange(t, dtype=jnp.float32)[:, None] * freqs[None, :]
            cos, sin = (jnp.cos(theta), jnp.sin(theta))
            x1, x2 = (x[..., 0::2], x[..., 1::2])
            r1 = x1 * cos - x2 * sin
            r2 = x1 * sin + x2 * cos
            return jnp.stack([r1, r2], axis=-1).reshape(x.shape)

        def _rmsnorm(x, w):
            return x * jax.lax.rsqrt(jnp.mean(x * x, axis=-1, keepdims=True) + EPS) * w
        Bx, Tx, C = x.shape
        q = x @ wq.T
        kv = x @ wkv.T
        k, v = (kv[..., :N_KV * D_HEAD], kv[..., N_KV * D_HEAD:])
        q = q.reshape(Bx, Tx, QPG, N_KV, D_HEAD).transpose(0, 2, 3, 1, 4)
        k = k.reshape(Bx, Tx, 1, N_KV, D_HEAD).transpose(0, 2, 3, 1, 4)
        v = v.reshape(Bx, Tx, 1, N_KV, D_HEAD).transpose(0, 2, 3, 1, 4)
        q = _rmsnorm(_rope(q), q_norm_w)
        k = _rmsnorm(_rope(k), k_norm_w)
        rows = jnp.arange(Tx)[:, None]
        cols = jnp.arange(Tx)[None, :]
        mask = (cols <= rows) & (rows - cols <= WINDOW)
        scale = 1.0 / math.sqrt(D_HEAD)
        scores = jnp.einsum('bqgtd,bqgsd->bqgts', q, k) * scale
        scores = jnp.where(mask[None, None, None], scores, NEG)
        attn = jax.nn.softmax(scores, axis=-1)
        out = jnp.einsum('bqgts,bqgsd->bqgtd', attn, v)
        out = out.transpose(0, 3, 1, 2, 4).reshape(Bx, Tx, QPG * N_KV * D_HEAD)
        return out @ wo.T

    def _L0_ffn_ref(x, route_id, Wi, bi, Wr, br, Ws, bs, Wo, bo):
        import jax, jax.numpy as jnp
        import numpy as np
        B, T, IN_DIM = (64, 64, 64)
        HID, OUT_DIM = (128, 64)
        N_LAYERS, N_EXPERTS, N_SHARED = (2, 16, 1)
        flat = x.reshape(-1, x.shape[-1])
        n_tok = flat.shape[0]
        route = jnp.repeat(route_id, n_tok // route_id.shape[0])
        h = jax.nn.relu(flat @ Wi.T + bi)
        n_layers, n_experts = (Wr.shape[0], Wr.shape[1])
        for l in range(n_layers):
            shared = (jnp.einsum('nd,shd->snh', h, Ws[l]) + bs[l][:, None, :]).mean(axis=0)
            routed = jnp.zeros_like(h)
            for e in range(n_experts):
                ye = h @ Wr[l, e].T + br[l, e]
                routed = routed + jnp.where((route == e)[:, None], ye, 0.0)
            h = jax.nn.relu(shared + routed + h)
        out = h @ Wo.T + bo
        return out.reshape(*x.shape[:-1], out.shape[-1])
    h = _L0_tok_ref(x, L0_tok_w, L0_tok_b, L0_tok_gamma, L0_tok_beta, L0_tok_alpha)
    h = h + _L0_attn_ref(_layernorm(h, axis=-1), L0_attn_wq, L0_attn_wkv, L0_attn_wo, L0_attn_q_norm_w, L0_attn_k_norm_w)
    h = h + _L0_ffn_ref(_layernorm(h, axis=-1), L0_ffn_route_id, L0_ffn_Wi, L0_ffn_bi, L0_ffn_Wr, L0_ffn_br, L0_ffn_Ws, L0_ffn_bs, L0_ffn_Wo, L0_ffn_bo)
    return h

_drawn_inputs = setup_inputs


def setup_inputs(seed=0):
    import zlib

    import numpy as np

    out = dict(_drawn_inputs(seed))
    spreads = {'L0_tok_gamma': (1.0, 0.2),
     'L0_tok_beta': (0.0, 0.1),
     'L0_attn_q_norm_w': (1.0, 0.6),
     'L0_attn_k_norm_w': (1.0, 0.6),
     'L0_ffn_bi': (0.0, 0.355),
     'L0_ffn_bo': (0.0, 0.1)}
    factors = {'L0_tok_alpha': 4.589,
     'L0_ffn_Wr': 5.099,
     'L0_ffn_br': 8.0,
     'L0_ffn_Ws': 5.155,
     'L0_ffn_bs': 7.737}
    for name, (base, spread) in spreads.items():
        noise = np.random.default_rng([zlib.crc32(name.encode()), seed]).standard_normal(out[name].shape)
        drawn = base * np.exp(spread * noise) if base else spread * noise
        out[name] = jnp.asarray(drawn.astype(out[name].dtype))
    for name, factor in factors.items():
        out[name] = (out[name] * factor).astype(out[name].dtype)
    return out
```

```python
from contextlib import ExitStack

import numpy as np
import concourse.bass as bass
from concourse import mybir

B, T_IN, C = 64, 125, 64
T, TP = 63, 64
TAPS = 5
NH, DH = 16, 64
HP = NH // 2
HID, NE, NL = 128, 16, 2
P = 128
PAIRS = B // 2
CH = 4
BPC = B // 2 // CH
PPC = PAIRS // CH
XW = 2 * (TP - 1) + TAPS + 1
WSLOT = HID + 1
FP = 4
FB = 2 * FP
FSTEPS = PAIRS // FP
NEG = -1.0e30
EPS_TOK, EPS_LN, EPS_RMS = 1e-3, 1e-5, 1.1920929e-07

C_ID, C_ONES, C_COS, C_SIN, C_MASK, C_EPS, C_END = 0, 128, 256, 320, 384, 448, 451
V_W, V_B, V_GAMMA, V_BETA, V_ALPHA, V_BI, V_BS, V_BR, V_END = 0, 5, 6, 7, 8, 9, 10, 12, 44
R_QW, R_KW, R_BO, R_END = 0, 64, 128, 192


def build(nc, x, consts, cols, rows, wq, wkv, wo, wi, wr, ws, wo2, route, out):
    f32, bf16, i32 = mybir.dt.float32, mybir.dt.bfloat16, mybir.dt.int32
    ALU, ACT, AX = mybir.AluOpType, mybir.ActivationFunctionType, mybir.AxisListType
    ctx = ExitStack()
    with ctx:
        def sb(name, shape, dt=f32):
            return ctx.enter_context(nc.sbuf_tensor(name, shape, dt))

        def sem(name):
            return ctx.enter_context(nc.semaphore(name))

        cst = sb("cst", [P, C_END])
        col = sb("col", [P, V_END])
        row = sb("row", [P, R_END])
        wq_sb = sb("wq_sb", [C, NH * DH])
        wkv_sb = sb("wkv_sb", [C, 2 * DH])
        wo_sb = sb("wo_sb", [P, HP * C])
        wi_sb = sb("wi_sb", [C, HID])
        ws_sb = sb("ws_sb", [P, NL, HID])
        wo2_sb = sb("wo2_sb", [HID, C])
        route_sb = sb("route_sb", [1, B], i32)
        experts = sb("experts", [P, NE, NL, WSLOT])
        ident_bf = sb("ident_bf", [P, P], bf16)
        mask_bf = sb("mask_bf", [P, HP, TP], bf16)
        taps = sb("taps", [P, TAPS, P])
        kw_row = sb("kw_row", [P, DH])
        ident = cst[:, C_ID:C_ID + P]
        ones_blk = cst[:, C_ONES:C_ONES + P]
        cos = cst[:, C_COS:C_COS + DH]
        sin = cst[:, C_SIN:C_SIN + DH]
        eps_tok, eps_ln, eps_rms = (cst[:, C_EPS + i:C_EPS + i + 1] for i in range(3))

        xin = sb("xin", [P, B // 2, XW])
        y = sb("y", [P, B // 2, TP])
        sq = sb("sq", [P, PPC * C])
        h = sb("h", [P, PAIRS, C])
        xh = sb("xh", [P, PAIRS, C])
        xT = sb("xT", [C, PAIRS, P])
        kc = sb("kc", [P, PPC, DH])
        ks = sb("ks", [P, PPC, DH])
        sqk = sb("sqk", [P, PPC, DH])
        khat = sb("khat", [P, PPC, DH])
        kT = sb("kT", [DH, PAIRS, P])
        vbd = sb("vbd", [P, PAIRS, 2, P])
        st = sb("st", [P, CH, 8, PPC])

        x_slot = sb("x_slot", [C, P])
        v_slot = sb("v_slot", [P, 2, P])
        qc = sb("qc", [P, NH, DH])
        qs = sb("qs", [P, NH, DH])
        qsq = sb("qsq", [P, NH, DH])
        qrot = sb("qrot", [P, NH, DH])
        qms = sb("qms", [P, 2, NH])
        qT = sb("qT", [DH, 2, NH, TP])
        pr = sb("pr", [P, 2, HP, TP])
        prm = sb("prm", [P, 2, 3, HP])
        pT = sb("pT", [P, 2, HP * TP])
        oT = sb("oT", [P, HP, 2, TP])

        w_slot = sb("w_slot", [P, FB, NL, WSLOT])
        f_st = sb("f_st", [P, 4, FP])
        f_sq = sq[:, 0:FP * C]
        f_x = kc[:, 0:FP, :]
        f_xT = sb("f_xT", [C, FP * P])
        f_h = [sb(f"f_h{i}", [HID, FP * P]) for i in range(3)]
        f_b = qc[:, 0:8, :].rearrange("p h d -> p (h d)")
        f_o = sb("f_o", [P, FP, C])

        ps = ctx.enter_context(nc.psum_tensor("ps", [P, 8, 512], f32))

        S = {n: sem(n) for n in (
            "ld_c", "ld_row", "ld_kv", "ld_q", "ld_o", "ld_ex", "ld_sh", "ld_ff", "ld_rt", "zeroed", "taps_ok", "kw_ok", "bf_ok", "ex_w", "ex_b", "vz",
            "conv", "y_raw", "y_sum", "mean", "y_cen", "y_sq", "y_sqs", "var", "y_std", "y_rs", "y_mul", "y_pos", "y_neg", "y_act",
            "tok", "h_ok", "h_sum", "h_cen", "h_sq", "h_sqs", "h_std", "h_rs", "xh_ok",
            "xTp", "xT_ok", "kv", "kcs", "k_sq", "v_ok", "k_rot", "k_sqs", "k_ln", "k_rs", "k_n1", "khat_ok", "kTp", "kT_ok",
            "ld_xs", "ld_vs", "q", "q_cs", "q_sq", "q_add", "q_sqs", "q_ln", "q_rs", "q_hat", "qTp", "qT_ok",
            "s_ok", "s_max", "s_sub", "s_exp", "s_sum", "s_rec", "s_prob", "pTp", "pT_ok", "o_ok", "oT_ok", "att", "att_ok",
            "ld_ws", "f_sum", "f_cen", "f_sq", "f_sqs", "f_ln", "f_rs", "f_xn", "f_xTp", "f_xT", "f_1p", "f_1",
            "f_lp", "f_lb", "f_l", "f_op", "f_ob", "f_o", "st_out")}
        ld_x = [sem(f"ld_x{j}") for j in range(CH)]
        ld_c = S["ld_c"]

        def need(eng, name, n):
            if not isinstance(n, int) or n > 0:
                eng.wait_ge(S[name], n)

        def value(eng, n):
            return n if isinstance(n, int) else eng.snap(eng.to_reg(n))

        block = ctx.enter_context(nc.Block())

        @block.sync
        def _(sp):
            sp.dma_start(cst[:], consts).then_inc(ld_c, 16)
            sp.dma_start(col[:], cols).then_inc(ld_c, 16)
            for j in range(CH):
                if j == 0:
                    sp.wait_ge(S["zeroed"], 1)
                sp.dma_start(xin[:, j * BPC:(j + 1) * BPC, 2:2 + T_IN],
                             x[:, j * BPC:(j + 1) * BPC, :]).then_inc(ld_x[j], 16)
            sp.dma_start(row[:], rows).then_inc(S["ld_row"], 16)
            sp.dma_start(wkv_sb[:], wkv).then_inc(S["ld_kv"], 16)
            sp.dma_start(wq_sb[:], wq).then_inc(S["ld_q"], 16)
            sp.dma_start(wo_sb[:], wo).then_inc(S["ld_o"], 16)
            sp.dma_start(experts[:, :, :, 0:HID], wr).then_inc(S["ld_ex"], 16)
            sp.dma_start(ws_sb[:], ws).then_inc(S["ld_sh"], 16)
            sp.dma_start(wi_sb[:], wi).then_inc(S["ld_ff"], 16)
            sp.dma_start(wo2_sb[:], wo2).then_inc(S["ld_ff"], 16)
            sp.dma_start(route_sb[:], route).then_inc(S["ld_rt"], 16)
            sp.wait_ge(S["xT_ok"], 2 * CH)
            sp.wait_ge(S["v_ok"], 8 * CH)

            def slots(p, loads=True, values=True):
                if loads:
                    need(sp, "q", 2 * p)
                    sp.dma_start(x_slot[:], xT[:, bass.ds(p, 1), :]).then_inc(S["ld_xs"], 16)
                if values:
                    need(sp, "o_ok", 2 * (p - 2))
                    sp.dma_start(v_slot[:], vbd[:, bass.ds(p - 2, 1), :, :]).then_inc(S["ld_vs"], 16)

            slots(0, values=False)
            slots(1, values=False)
            with sp.Fori(2, PAIRS) as p:
                slots(p)
            slots(PAIRS, loads=False)
            slots(PAIRS + 1, loads=False)

            sp.wait_ge(S["ld_rt"], 16)
            sp.wait_ge(S["ex_w"], 2)
            sp.wait_ge(S["ex_b"], 1)

            def ff_slots(s):
                need(sp, "f_lp", 2 * s)
                need(sp, "f_lb", 2 * s)
                for k in range(FB):
                    half, g2 = (k // 2) % 2, k // 4
                    e = sp.value_load(route_sb[0:1, bass.ds(s * FP + (half * (B // 2) + 2 * g2 + k % 2), 1)],
                                      min_val=0, max_val=NE - 1)
                    sp.dma_start(w_slot[:, k, :, :], experts[:, bass.ds(e, 1), :, :]).then_inc(S["ld_ws"], 16)

            ff_slots(0)
            with sp.Fori(1, FSTEPS) as s:
                ff_slots(s)
                sp.wait_ge(S["f_o"], s)
                sp.dma_start(out[:, bass.ds(s * FP - FP, FP), :], f_o[:]).then_inc(S["st_out"], 16)
            sp.wait_ge(S["f_o"], FSTEPS)
            sp.dma_start(out[:, PAIRS - FP:, :], f_o[:]).then_inc(S["st_out"], 16)
            sp.wait_ge(S["st_out"], 16 * FSTEPS)

        @block.gpsimd
        def _(pool):
            nc.gpsimd.memset(xin[:, :, 0:2], 0.0)
            nc.gpsimd.memset(xin[:, :, 2 + T_IN:XW], 0.0).then_inc(S["zeroed"], 1)
            nc.gpsimd.memset(vbd[:], 0.0).then_inc(S["vz"], 1)
            pool.wait_ge(ld_c, 32)
            pool.wait_ge(S["ld_sh"], 16)
            pool.wait_ge(S["ld_ex"], 16)
            nc.gpsimd.tensor_tensor(ws_sb[:], ws_sb[:], ident.unsqueeze(1).broadcast_to([P, NL, HID]),
                                    ALU.add).then_inc(S["ex_w"], 1)
            nc.gpsimd.tensor_tensor(experts[:, :, :, HID],
                                    col[:, V_BR:V_BR + NL * NE].rearrange("p (l e) -> p e l", l=NL),
                                    col[:, V_BS:V_BS + NL].unsqueeze(1).broadcast_to([P, NE, NL]),
                                    ALU.add).then_inc(S["ex_b"], 1)
            pool.wait_ge(S["ex_w"], 1)
            nc.gpsimd.tensor_tensor(experts[:, :, :, 0:HID], experts[:, :, :, 0:HID],
                                    ws_sb[:].unsqueeze(1).broadcast_to([P, NE, NL, HID]),
                                    ALU.add).then_inc(S["ex_w"], 1)
            for j in range(CH):
                pool.wait_ge(S["kcs"], 2 * (j + 1))
                need(pool, "k_n1", j)
                nc.gpsimd.tensor_tensor(kc[:], kc[:], ks[:], ALU.add).then_inc(S["k_rot"], 1)

            def stages(p, scale=True, norm=True):
                if scale:
                    for i in range(2):
                        hs = slice(i * 8, i * 8 + 8)
                        pool.wait_ge(S["q_cs"], 2 * p + i + 1)
                        nc.gpsimd.tensor_tensor(qc[:, hs], qc[:, hs], qs[:, hs], ALU.add).then_inc(S["q_add"], 1)
                    pool.wait_ge(S["q_add"], 2 * p + 2)
                    pool.wait_ge(S["q_rs"], p + 1)
                    need(pool, "qTp", 4 * p)
                    nc.gpsimd.tensor_tensor(qrot[:], qc[:], qms[:, 1, :].unsqueeze(2).broadcast_to([P, NH, DH]),
                                            ALU.mult).then_inc(S["q_hat"], 1)
                if norm:
                    for b in range(2):
                        pool.wait_ge(S["s_rec"], 2 * (p - 1) + b + 1)
                        nc.gpsimd.tensor_tensor(pr[:, b], pr[:, b],
                                                prm[:, b, 2, :].unsqueeze(2).broadcast_to([P, HP, TP]),
                                                ALU.mult).then_inc(S["s_prob"], 1)

            stages(0, norm=False)
            with pool.Fori(1, PAIRS) as p:
                stages(p)
            stages(PAIRS, scale=False)

            def ff(s):
                pool.wait_ge(S["f_ob"], s + 1)
                nc.gpsimd.tensor_tensor(f_o[:], f_o[:], h[:, bass.ds(s * FP, FP), :], ALU.add).then_inc(S["f_o"], 1)

            with pool.Fori(0, FSTEPS) as s:
                ff(s)

        @block.scalar
        def _(act):
            def copy(o, i, name):
                nc.scalar.activation(o, i, ACT.Copy).then_inc(S[name], 1)

            act.wait_ge(ld_c, 32)
            copy(ident_bf[:], ident, "bf_ok")
            copy(mask_bf[:], cst[:, C_MASK:C_MASK + TP].unsqueeze(1).broadcast_to([P, HP, TP]), "bf_ok")

            for step in range(CH + 3):
                j = step
                if j < CH:
                    act.wait_ge(S["conv"], j + 1)
                    nc.scalar.activation(y[:, j * BPC:(j + 1) * BPC, :],
                                         ps[:, 0, :].rearrange("p (b t) -> p b t", t=TP),
                                         ACT.Identity, bias=col[:, V_B:V_B + 1]).then_inc(S["y_raw"], 1)
                j = step - 1
                if 0 <= j < CH:
                    yj = y[:, j * BPC:(j + 1) * BPC, :]
                    act.wait_ge(S["y_cen"], j + 1)
                    need(act, "y_sqs", j)
                    need(act, "h_sqs", j - 1)
                    nc.scalar.activation(sq[:].rearrange("p (b t) -> p b t", t=TP), yj,
                                         ACT.Square).then_inc(S["y_sq"], 1)
                    act.wait_ge(S["var"], j + 1)
                    nc.scalar.activation(st[:, j, 2], ps[:, 1, BPC:2 * BPC], ACT.Ln,
                                         bias=eps_tok).then_inc(S["y_std"], 1)
                    act.wait_ge(S["y_std"], j + 1)
                    nc.scalar.activation(st[:, j, 3], st[:, j, 2], ACT.Exp, scale=-0.5).then_inc(S["y_rs"], 1)
                    act.wait_ge(S["y_mul"], 2 * (j + 1))
                    nc.scalar.activation(h[:, j * BPC:(j + 1) * BPC, :], yj, ACT.Relu,
                                         bias=col[:, V_BETA:V_BETA + 1]).then_inc(S["y_pos"], 1)
                j = step - 2
                if 0 <= j < CH:
                    hj = h[:, j * PPC:(j + 1) * PPC, :]
                    act.wait_ge(S["tok"], j + 1)
                    copy(hj, ps[:, 2, :].rearrange("p (n c) -> p n c", c=C), "h_ok")
                    act.wait_ge(S["h_cen"], 2 * (j + 1))
                    need(act, "y_sqs", min(j + 2, CH))
                    nc.scalar.activation(sq[:].rearrange("p (n c) -> p n c", c=C),
                                         xh[:, j * PPC:(j + 1) * PPC, :], ACT.Square).then_inc(S["h_sq"], 1)
                    act.wait_ge(S["h_sqs"], j + 1)
                    nc.scalar.activation(st[:, j, 6], st[:, j, 6], ACT.Ln, scale=1.0 / C,
                                         bias=eps_ln).then_inc(S["h_std"], 1)
                    act.wait_ge(S["h_std"], j + 1)
                    nc.scalar.activation(st[:, j, 7], st[:, j, 6], ACT.Exp, scale=-0.5).then_inc(S["h_rs"], 1)
                j = step - 3
                if j >= 0:
                    for r in range(2):
                        act.wait_ge(S["xTp"], 2 * j + r + 1)
                        p0 = j * PPC + 4 * r
                        copy(xT[:, p0:p0 + 4, :], ps[0:C, 3 + r, :].rearrange("c (n t) -> c n t", t=P), "xT_ok")
                    for r in range(2):
                        act.wait_ge(S["kv"], 2 * j + r + 1)
                        act.wait_ge(S["kcs"], 2 * j + r + 1)
                        need(act, "k_sqs", j)
                        kv = ps[:, 5 + r, :].rearrange("p (n f) -> p n f", f=2 * DH)
                        nc.scalar.activation(sqk[:, 4 * r:4 * r + 4, :], kv[:, :, 0:DH],
                                             ACT.Square).then_inc(S["k_sq"], 1)
                        act.wait_ge(S["vz"], 1)
                        p0 = j * PPC + 4 * r
                        for b in range(2):
                            for a in range(2):
                                copy(vbd[a * DH:(a + 1) * DH, p0:p0 + 4, b, a * DH:(a + 1) * DH],
                                     kv[b * TP:(b + 1) * TP, :, DH:], "v_ok")
                    act.wait_ge(S["k_sqs"], j + 1)
                    nc.scalar.activation(st[:, j, 0], st[:, j, 4], ACT.Ln, scale=1.0 / DH,
                                         bias=eps_rms).then_inc(S["k_ln"], 1)
                    act.wait_ge(S["k_ln"], j + 1)
                    nc.scalar.activation(st[:, j, 1], st[:, j, 0], ACT.Exp, scale=-0.5).then_inc(S["k_rs"], 1)
                    for r in range(2):
                        act.wait_ge(S["kTp"], 2 * j + r + 1)
                        p0 = j * PPC + 4 * r
                        copy(kT[:, p0:p0 + 4, :], ps[0:DH, 7, :].rearrange("c (n t) -> c n t", t=P), "kT_ok")

            def stages(p, pa=True, pb=True, pc=True):
                if pb:
                    for r in range(4):
                        act.wait_ge(S["qTp"], 4 * (p - 1) + r + 1)
                        if r == 0:
                            need(act, "s_ok", 2 * (p - 1))
                        copy(qT[:, :, 4 * r:4 * r + 4, :],
                             ps[0:DH, 2 + r % 2, :].rearrange("d (n b t) -> d b n t", b=2, t=TP), "qT_ok")
                if pa:
                    for i in range(2):
                        act.wait_ge(S["q_cs"], 2 * p + i + 1)
                        if i == 0:
                            need(act, "q_sqs", p)
                        nc.scalar.activation(qsq[:, i * 8:i * 8 + 8, :],
                                             ps[:, i, :].rearrange("p (n d) -> p n d", d=DH),
                                             ACT.Square).then_inc(S["q_sq"], 1)
                for b in range(2):
                    if pc:
                        act.wait_ge(S["pTp"], 2 * (p - 2) + b + 1)
                        need(act, "o_ok", 2 * (p - 3) + b + 1)
                        copy(pT[:, b, :], ps[:, 6, :], "pT_ok")
                    if pb:
                        act.wait_ge(S["s_sub"], 2 * (p - 1) + b + 1)
                        nc.scalar.activation(pr[:, b], pr[:, b], ACT.Exp).then_inc(S["s_exp"], 1)
                    if pa and b == 0:
                        act.wait_ge(S["q_sqs"], p + 1)
                        nc.scalar.activation(qms[:, 1, :], qms[:, 0, :], ACT.Ln, scale=1.0 / DH,
                                             bias=eps_rms).then_inc(S["q_ln"], 1)
                        act.wait_ge(S["q_ln"], p + 1)
                        nc.scalar.activation(qms[:, 1, :], qms[:, 1, :], ACT.Exp, scale=-0.5).then_inc(S["q_rs"], 1)
                    if pc:
                        act.wait_ge(S["o_ok"], 2 * (p - 2) + b + 1)
                        if b == 0:
                            need(act, "att", p - 2)
                        copy(oT[:, :, b, :], ps[:, 7, :].rearrange("p (n t) -> p n t", t=TP), "oT_ok")

            stages(0, pb=False, pc=False)
            stages(1, pc=False)
            stages(2)
            with act.Fori(3, PAIRS) as p:
                stages(p)
            stages(PAIRS, pa=False)
            stages(PAIRS + 1, pa=False, pb=False)

            def ff(s):
                act.wait_ge(S["f_cen"], 2 * s + 2)
                nc.scalar.activation(f_sq.rearrange("p (n c) -> p n c", c=C), f_x, ACT.Square).then_inc(S["f_sq"], 1)
                act.wait_ge(S["f_sqs"], s + 1)
                nc.scalar.activation(f_st[:, 2, :], f_st[:, 1, :], ACT.Ln, scale=1.0 / C,
                                     bias=eps_ln).then_inc(S["f_ln"], 1)
                act.wait_ge(S["f_ln"], s + 1)
                nc.scalar.activation(f_st[:, 3, :], f_st[:, 2, :], ACT.Exp, scale=-0.5).then_inc(S["f_rs"], 1)
                act.wait_ge(S["f_xTp"], s + 1)
                need(act, "f_1p", s)
                copy(f_xT[:], ps[0:C, 0, :], "f_xT")
                act.wait_ge(S["f_1p"], s + 1)
                need(act, "f_lp", 2 * s)
                nc.scalar.activation(f_h[0][:], ps[:, 1, :], ACT.Relu, bias=col[:, V_BI:V_BI + 1]).then_inc(S["f_1"], 1)
                for l in range(NL):
                    act.wait_ge(S["f_lb"], 2 * s + l + 1)
                    nc.scalar.activation(f_h[l + 1][:], f_b, ACT.Relu).then_inc(S["f_l"], 1)

            with act.Fori(0, FSTEPS) as s:
                ff(s)

        @block.vector
        def _(dve):
            dve.wait_ge(ld_c, 32)
            for k in range(TAPS):
                last = nc.vector.tensor_scalar(taps[:, k, :], ident, col[:, V_W + k:V_W + k + 1], None, ALU.mult)
            last.then_inc(S["taps_ok"], 1)
            dve.wait_ge(S["ld_row"], 16)
            nc.vector.scalar_tensor_tensor(out=kw_row[:], in0=row[:, R_QW:R_QW + DH], scalar=float(DH) ** -0.5,
                                           in1=row[:, R_KW:R_KW + DH], op0=ALU.mult,
                                           op1=ALU.mult).then_inc(S["kw_ok"], 1)

            def wide(v, n, w):
                return v.unsqueeze(2).broadcast_to([P, n, w])

            for step in range(CH + 3):
                j = step
                if j < CH:
                    dve.wait_ge(S["y_raw"], j + 1)
                    nc.vector.reduce_sum(st[:, j, 0], y[:, j * BPC:(j + 1) * BPC, 0:T], AX.X).then_inc(S["y_sum"], 1)
                j = step - 1
                if 0 <= j < CH:
                    yj = y[:, j * BPC:(j + 1) * BPC, :]
                    dve.wait_ge(S["mean"], j + 1)
                    nc.vector.tensor_tensor(yj, yj, wide(ps[:, 1, 0:BPC], BPC, TP), ALU.subtract).then_inc(S["y_cen"], 1)
                    dve.wait_ge(S["y_sq"], j + 1)
                    nc.vector.reduce_sum(st[:, j, 1], sq[:].rearrange("p (b t) -> p b t", t=TP)[:, :, 0:T],
                                         AX.X).then_inc(S["y_sqs"], 1)
                    dve.wait_ge(S["y_rs"], j + 1)
                    nc.vector.tensor_scalar(st[:, j, 3], st[:, j, 3], col[:, V_GAMMA:V_GAMMA + 1], None,
                                            ALU.mult).then_inc(S["y_mul"], 1)
                    dve.wait_ge(S["y_mul"], 2 * j + 1)
                    nc.vector.tensor_tensor(yj, yj, wide(st[:, j, 3], BPC, TP), ALU.mult).then_inc(S["y_mul"], 1)
                    dve.wait_ge(S["y_pos"], j + 1)
                    nc.vector.tensor_scalar(yj, yj, col[:, V_BETA:V_BETA + 1], 0.0, ALU.add,
                                            ALU.min).then_inc(S["y_neg"], 1)
                    dve.wait_ge(S["y_neg"], j + 1)
                    nc.vector.scalar_tensor_tensor(out=yj, in0=yj, scalar=col[:, V_ALPHA:V_ALPHA + 1],
                                                   in1=h[:, j * BPC:(j + 1) * BPC, :], op0=ALU.mult,
                                                   op1=ALU.add).then_inc(S["y_act"], 1)
                j = step - 2
                if 0 <= j < CH:
                    hj, xj = h[:, j * PPC:(j + 1) * PPC, :], xh[:, j * PPC:(j + 1) * PPC, :]
                    dve.wait_ge(S["h_ok"], j + 1)
                    nc.vector.reduce_sum(st[:, j, 4], hj, AX.X).then_inc(S["h_sum"], 1)
                    dve.wait_ge(S["h_sum"], j + 1)
                    nc.vector.tensor_scalar(st[:, j, 5], st[:, j, 4], 1.0 / C, None, ALU.mult).then_inc(S["h_cen"], 1)
                    dve.wait_ge(S["h_cen"], 2 * j + 1)
                    nc.vector.tensor_tensor(xj, hj, wide(st[:, j, 5], PPC, C), ALU.subtract).then_inc(S["h_cen"], 1)
                    dve.wait_ge(S["h_sq"], j + 1)
                    nc.vector.reduce_sum(st[:, j, 6], sq[:].rearrange("p (n c) -> p n c", c=C),
                                         AX.X).then_inc(S["h_sqs"], 1)
                    dve.wait_ge(S["h_rs"], j + 1)
                    nc.vector.tensor_tensor(xj, xj, wide(st[:, j, 7], PPC, C), ALU.mult).then_inc(S["xh_ok"], 1)
                j = step - 3
                if j >= 0:
                    need(dve, "k_n1", j)
                    for r in range(2):
                        dve.wait_ge(S["kv"], 2 * j + r + 1)
                        k4 = ps[:, 5 + r, :].rearrange("p (n f) -> p n f", f=2 * DH)
                        n4 = slice(4 * r, 4 * r + 4)
                        nc.vector.tensor_tensor(kc[:, n4, :], k4[:, :, 0:DH],
                                                cos.unsqueeze(1).broadcast_to([P, 4, DH]), ALU.mult)
                        nc.vector.tensor_tensor(ks[:, n4, 0:32], k4[:, :, 32:64],
                                                sin[:, 0:32].unsqueeze(1).broadcast_to([P, 4, 32]), ALU.mult)
                        nc.vector.tensor_tensor(ks[:, n4, 32:64], k4[:, :, 0:32],
                                                sin[:, 32:64].unsqueeze(1).broadcast_to([P, 4, 32]),
                                                ALU.mult).then_inc(S["kcs"], 1)
                    dve.wait_ge(S["k_sq"], 2 * (j + 1))
                    dve.wait_ge(S["h_cen"], 2 * (j + 1))
                    nc.vector.reduce_sum(st[:, j, 4], sqk[:], AX.X).then_inc(S["k_sqs"], 1)
                    dve.wait_ge(S["k_rs"], j + 1)
                    dve.wait_ge(S["k_rot"], j + 1)
                    need(dve, "kTp", 2 * j)
                    nc.vector.tensor_tensor(khat[:], kc[:], wide(st[:, j, 1], PPC, DH), ALU.mult).then_inc(S["k_n1"], 1)
                    dve.wait_ge(S["k_n1"], j + 1)
                    dve.wait_ge(S["kw_ok"], 1)
                    nc.vector.tensor_tensor(khat[:], khat[:], kw_row[:].unsqueeze(1).broadcast_to([P, PPC, DH]),
                                            ALU.mult).then_inc(S["khat_ok"], 1)

            def probs_sum(p, b):
                dve.wait_ge(S["s_exp"], 2 * (p - 1) + b + 1)
                nc.vector.reduce_sum(prm[:, b, 1, :], pr[:, b], AX.X).then_inc(S["s_sum"], 1)
                dve.wait_ge(S["s_sum"], 2 * (p - 1) + b + 1)
                nc.vector.reciprocal(prm[:, b, 2, :], prm[:, b, 1, :]).then_inc(S["s_rec"], 1)

            def stages(p, pa=True, pb=True, pd=True):
                if pd:
                    dve.wait_ge(S["att"], p - 2)
                    hp = h[:, bass.ds(p - 3, 1), :]
                    nc.vector.tensor_tensor(hp, hp, ps[:, 6:7, 0:C], ALU.add).then_inc(S["att_ok"], 1)
                if pa:
                    for i in range(2):
                        dve.wait_ge(S["q"], 2 * p + i + 1)
                        if i == 0:
                            need(dve, "q_hat", p)
                        hs = slice(8 * i, 8 * i + 8)
                        q8 = ps[:, i, :].rearrange("p (n d) -> p n d", d=DH)
                        nc.vector.tensor_tensor(qc[:, hs, :], q8, cos.unsqueeze(1).broadcast_to([P, 8, DH]), ALU.mult)
                        nc.vector.tensor_tensor(qs[:, hs, 0:32], q8[:, :, 32:64],
                                                sin[:, 0:32].unsqueeze(1).broadcast_to([P, 8, 32]), ALU.mult)
                        nc.vector.tensor_tensor(qs[:, hs, 32:64], q8[:, :, 0:32],
                                                sin[:, 32:64].unsqueeze(1).broadcast_to([P, 8, 32]),
                                                ALU.mult).then_inc(S["q_cs"], 1)
                for b in range(2):
                    if pb:
                        n = 2 * (p - 1) + b + 1
                        dve.wait_ge(S["s_ok"], n)
                        s_ps = ps[:, 4 + b, :].rearrange("p (n s) -> p n s", s=TP)
                        nc.vector.reduce_max(prm[:, b, 0, :], s_ps, AX.X).then_inc(S["s_max"], 1)
                        dve.wait_ge(S["s_max"], n)
                        need(dve, "pTp", n - 2)
                        nc.vector.tensor_tensor(pr[:, b], s_ps, wide(prm[:, b, 0, :], HP, TP),
                                                ALU.subtract).then_inc(S["s_sub"], 1)
                    if pa and b == 0:
                        dve.wait_ge(S["q_sq"], 2 * p + 2)
                        nc.vector.reduce_sum(qms[:, 0, :], qsq[:], AX.X).then_inc(S["q_sqs"], 1)
                if pb:
                    for b in range(2):
                        probs_sum(p, b)

            stages(0, pb=False, pd=False)
            stages(1, pd=False)
            stages(2, pd=False)
            with dve.Fori(3, PAIRS) as p:
                stages(p)
            stages(PAIRS, pa=False)
            stages(PAIRS + 1, pa=False, pb=False)
            stages(PAIRS + 2, pa=False, pb=False)

            def ff(s):
                hs = h[:, bass.ds(s * FP, FP), :]
                if isinstance(s, int) and s == 0:
                    dve.wait_ge(S["att_ok"], PAIRS)
                nc.vector.reduce_sum(f_st[:, 0, :], hs, AX.X).then_inc(S["f_sum"], 1)
                dve.wait_ge(S["f_sum"], s + 1)
                nc.vector.tensor_scalar(f_st[:, 1, :], f_st[:, 0, :], 1.0 / C, None, ALU.mult).then_inc(S["f_cen"], 1)
                dve.wait_ge(S["f_cen"], 2 * s + 1)
                need(dve, "f_xTp", s)
                nc.vector.tensor_tensor(f_x, hs, wide(f_st[:, 1, :], FP, C), ALU.subtract).then_inc(S["f_cen"], 1)
                dve.wait_ge(S["f_cen"], 2 * s + 2)
                dve.wait_ge(S["f_sq"], s + 1)
                nc.vector.reduce_sum(f_st[:, 1, :], f_sq.rearrange("p (n c) -> p n c", c=C), AX.X).then_inc(S["f_sqs"], 1)
                dve.wait_ge(S["f_rs"], s + 1)
                nc.vector.tensor_tensor(f_x, f_x, wide(f_st[:, 3, :], FP, C), ALU.mult).then_inc(S["f_xn"], 1)
                for l in range(NL):
                    dve.wait_ge(S["f_lp"], 2 * s + l + 1)
                    if l == 0:
                        need(dve, "f_l", 2 * s)
                    else:
                        dve.wait_ge(S["f_l"], 2 * s + 1)
                    nc.vector.tensor_tensor(f_b.rearrange("p (b t) -> p b t", t=TP),
                                            ps[:, 2 + l, :].rearrange("p (b t) -> p b t", t=TP),
                                            w_slot[:, :, l, HID:].broadcast_to([P, FB, TP]),
                                            ALU.add).then_inc(S["f_lb"], 1)
                dve.wait_ge(S["f_op"], s + 1)
                need(dve, "st_out", 16 * s)
                nc.vector.tensor_tensor(f_o[:], ps[:, 4, 0:FP * C].rearrange("p (n c) -> p n c", c=C),
                                        row[:, R_BO:R_BO + C].unsqueeze(1).broadcast_to([P, FP, C]),
                                        ALU.add).then_inc(S["f_ob"], 1)

            ff(0)
            with dve.Fori(1, FSTEPS) as s:
                ff(s)

        @block.tensor
        def _(pe):
            mm = nc.tensor.matmul
            pe.wait_ge(S["taps_ok"], 1)
            pe.wait_ge(S["zeroed"], 1)
            for step in range(CH + 3):
                j = step
                if j < CH:
                    pe.wait_ge(ld_x[j], 16)
                    need(pe, "y_raw", j)
                    for k in range(TAPS):
                        last = mm(ps[:, 0, :], taps[:, k, :],
                                  xin[:, j * BPC:(j + 1) * BPC, k:k + 2 * TP - 1:2], start=k == 0, stop=k == TAPS - 1)
                    last.then_inc(S["conv"], 1)
                j = step - 1
                if 0 <= j < CH:
                    pe.wait_ge(S["y_sum"], j + 1)
                    need(pe, "y_std", j)
                    mm(ps[:, 1, 0:BPC], ones_blk, st[:, j, 0], start=True, stop=True).then_inc(S["mean"], 1)
                    pe.wait_ge(S["y_sqs"], j + 1)
                    pe.wait_ge(S["y_cen"], j + 1)
                    mm(ps[:, 1, BPC:2 * BPC], ones_blk, st[:, j, 1], start=True, stop=True).then_inc(S["var"], 1)
                j = step - 2
                if 0 <= j < CH:
                    pe.wait_ge(S["y_act"], j + 1)
                    need(pe, "h_ok", j)
                    for g in range(4):
                        b0 = j * BPC + 2 * g
                        last = nc.tensor.transpose(ps[:, 2, g * P:(g + 1) * P], y[:, b0:b0 + 2, :], ident)
                    last.then_inc(S["tok"], 1)
                j = step - 3
                if j >= 0:
                    pe.wait_ge(S["xh_ok"], j + 1)
                    need(pe, "xT_ok", 2 * j)
                    for r in range(2):
                        for n in range(4):
                            last = nc.tensor.transpose(ps[0:C, 3 + r, n * P:(n + 1) * P], xh[:, j * PPC + 4 * r + n, :], ident)
                        last.then_inc(S["xTp"], 1)
                    pe.wait_ge(S["ld_kv"], 16)
                    need(pe, "v_ok", 8 * j)
                    for r in range(2):
                        pe.wait_ge(S["xT_ok"], 2 * j + r + 1)
                        for n in range(4):
                            last = mm(ps[:, 5 + r, n * P:(n + 1) * P], xT[:, j * PPC + 4 * r + n, :], wkv_sb[:],
                                      start=True, stop=True)
                        last.then_inc(S["kv"], 1)
                    pe.wait_ge(S["khat_ok"], j + 1)
                    for r in range(2):
                        need(pe, "kT_ok", 2 * j + r)
                        for n in range(4):
                            last = nc.tensor.transpose(ps[0:DH, 7, n * P:(n + 1) * P], khat[:, 4 * r + n, :], ident)
                        last.then_inc(S["kTp"], 1)

            pe.wait_ge(S["kT_ok"], 2 * CH)
            pe.wait_ge(S["bf_ok"], 2)
            pe.wait_ge(S["ld_q"], 16)
            pe.wait_ge(S["ld_o"], 16)

            def project(p, i):
                if i == 0:
                    pe.wait_ge(S["ld_xs"], 16 * p + 16)
                need(pe, "q_sq", 2 * (p - 1) + i + 1)
                mm(ps[:, i, :], x_slot[:], wq_sb[:, i * 512:(i + 1) * 512], start=True, stop=True).then_inc(S["q"], 1)

            def transpose_q(p, r):
                if r == 0:
                    pe.wait_ge(S["q_hat"], p + 1)
                freed = value(pe, 4 * p + r - 1)
                pe.wait_ge(ld_c, 32)
                need(pe, "qT_ok", freed)
                for n in range(4):
                    last = nc.tensor.transpose(ps[0:DH, 2 + r % 2, n * P:(n + 1) * P], qrot[:, 4 * r + n, :], ident)
                last.then_inc(S["qTp"], 1)

            def scores(p, b):
                if b == 0:
                    pe.wait_ge(S["qT_ok"], 4 * p + 4)
                need(pe, "s_sub", 2 * (p - 1) + b + 1)
                mm(ps[:, 4 + b, :], ident_bf[:], mask_bf[:], start=True, stop=False)
                for n in range(HP):
                    last = mm(ps[:, 4 + b, n * TP:(n + 1) * TP], qT[:, b, 2 * n:2 * n + 2, :],
                              kT[:, bass.ds(p, 1), b * TP:(b + 1) * TP], start=False, stop=n == HP - 1)
                last.then_inc(S["s_ok"], 1)

            def transpose_p(p, b):
                pe.wait_ge(S["s_prob"], 2 * p + b + 1)
                need(pe, "pT_ok", 2 * p + b)
                if b == 0:
                    need(pe, "att_ok", p)
                for n in range(4):
                    last = nc.tensor.transpose(ps[:, 6, n * P:(n + 1) * P], pr[:, b, 2 * n:2 * n + 2, :], ident)
                last.then_inc(S["pTp"], 1)

            def values(p, b):
                if b == 0:
                    pe.wait_ge(S["ld_vs"], 16 * p + 16)
                pe.wait_ge(S["pT_ok"], 2 * p + b + 1)
                need(pe, "oT_ok", 2 * p + b)
                mm(ps[:, 7, :], v_slot[:, b, :], pT[:, b, :], start=True, stop=True).then_inc(S["o_ok"], 1)

            def output(p):
                pe.wait_ge(S["oT_ok"], 2 * p + 2)
                pe.wait_ge(S["pT_ok"], 2 * p + 2)
                for n in range(HP):
                    last = mm(ps[:, 6, 0:C], oT[:, n, :, :], wo_sb[:, n * C:(n + 1) * C], start=n == 0, stop=n == HP - 1)
                last.then_inc(S["att"], 1)

            def stages(p, pa=True, pb=True, pc=True, pd=True):
                if pb:
                    transpose_q(p - 1, 0)
                    transpose_q(p - 1, 1)
                if pd:
                    output(p - 3)
                if pa:
                    project(p, 0)
                if pb:
                    transpose_q(p - 1, 2)
                    transpose_q(p - 1, 3)
                if pc:
                    transpose_p(p - 2, 0)
                if pa:
                    project(p, 1)
                if pc:
                    values(p - 2, 0)
                if pb:
                    scores(p - 1, 0)
                if pc:
                    transpose_p(p - 2, 1)
                if pb:
                    scores(p - 1, 1)
                if pc:
                    values(p - 2, 1)

            stages(0, pb=False, pc=False, pd=False)
            stages(1, pc=False, pd=False)
            stages(2, pd=False)
            with pe.Fori(3, PAIRS) as p:
                stages(p)
            stages(PAIRS, pa=False)
            stages(PAIRS + 1, pa=False, pb=False)
            stages(PAIRS + 2, pa=False, pb=False, pc=False)

            pe.wait_ge(S["ld_ff"], 32)
            pe.wait_ge(S["att_ok"], PAIRS)

            def ff(s):
                normed = value(pe, s + 1)
                pe.wait_ge(ld_c, 32)
                pe.wait_ge(S["f_xn"], normed)
                for n in range(FP):
                    last = nc.tensor.transpose(ps[0:C, 0, n * P:(n + 1) * P], f_x[:, n, :], ident)
                last.then_inc(S["f_xTp"], 1)
                pe.wait_ge(S["f_xT"], s + 1)
                mm(ps[:, 1, :], wi_sb[:], f_xT[:], start=True, stop=True).then_inc(S["f_1p"], 1)
                pe.wait_ge(S["ld_ws"], 16 * FB * s + 16 * FB)
                for l in range(NL):
                    if l == 0:
                        pe.wait_ge(S["f_1"], s + 1)
                    else:
                        pe.wait_ge(S["f_l"], 2 * s + 1)
                    for b in range(FB):
                        last = mm(ps[:, 2 + l, b * TP:(b + 1) * TP], w_slot[:, b, l, 0:HID],
                                  f_h[l][:, b * TP:(b + 1) * TP], start=True, stop=True)
                    last.then_inc(S["f_lp"], 1)
                pe.wait_ge(S["f_l"], 2 * s + 2)
                need(pe, "f_ob", s)
                for n in range(FP):
                    last = mm(ps[:, 4, n * C:(n + 1) * C], f_h[2][:, n * P:(n + 1) * P], wo2_sb[:], start=True, stop=True)
                last.then_inc(S["f_op"], 1)

            ff(0)
            with pe.Fori(1, FSTEPS) as s:
                ff(s)


def shape_constants():
    c = np.zeros((P, C_END), np.float32)
    c[:, C_ID:C_ID + P] = np.eye(P, dtype=np.float32)
    c[:, C_ONES:C_ONES + P] = np.kron(np.eye(2), np.ones((C, C))) / (T * C)
    half = DH // 2
    freqs = np.float32(10000.0) ** (np.float32(-2.0) * np.arange(half, dtype=np.float32) / np.float32(DH))
    theta = np.tile(np.arange(TP, dtype=np.float32), 2)[:, None] * freqs[None, :]
    c[:, C_COS:C_COS + DH] = np.tile(np.cos(theta), 2)
    c[:, C_SIN:C_SIN + half] = -np.sin(theta)
    c[:, C_SIN + half:C_SIN + DH] = np.sin(theta)
    t, s = np.tile(np.arange(TP), 2)[:, None], np.arange(TP)[None, :]
    c[:, C_MASK:C_MASK + TP] = np.where(s <= t, 0.0, NEG)
    c[:, C_EPS:C_EPS + 3] = [EPS_TOK, EPS_LN, EPS_RMS]
    return c


def kernel(x, L0_tok_w, L0_tok_b, L0_tok_gamma, L0_tok_beta, L0_tok_alpha, L0_attn_wq, L0_attn_wkv, L0_attn_wo,
           L0_attn_q_norm_w, L0_attn_k_norm_w, L0_ffn_route_id, L0_ffn_Wi, L0_ffn_bi, L0_ffn_Wr, L0_ffn_br,
           L0_ffn_Ws, L0_ffn_bs, L0_ffn_Wo, L0_ffn_bo):
    import concourse.bacc as bacc
    from concourse.bass_utils import run_bass_kernel_spmd

    perm = np.concatenate([np.arange(0, DH, 2), np.arange(1, DH, 2)])
    wide = lambda v: np.broadcast_to(v, (P, v.shape[-1]))
    col = lambda v: np.tile(v, P // v.shape[0])[:, None]
    wq = L0_attn_wq.reshape(NH, DH, C)[:, perm].reshape(NH * DH, C)
    arrays = {
        "x_in": x.reshape(2, B // 2, T_IN, C).transpose(0, 3, 1, 2).reshape(P, B // 2, T_IN),
        "consts": shape_constants(),
        "cols": np.concatenate(
            [col(L0_tok_w[k, 0]) for k in range(TAPS)]
            + [col(v) for v in (L0_tok_b, L0_tok_gamma, L0_tok_beta, L0_tok_alpha, L0_ffn_bi)]
            + [L0_ffn_bs[:, 0].T, L0_ffn_br.reshape(NL * NE, HID).T], axis=1),
        "rows": np.concatenate([wide(L0_attn_q_norm_w[perm]), wide(L0_attn_k_norm_w[perm]), wide(L0_ffn_bo)], axis=1),
        "wq": wq.T,
        "wkv": np.concatenate([L0_attn_wkv[:DH][perm], L0_attn_wkv[DH:]]).T,
        "wo": L0_attn_wo.reshape(C, 4, 2, 2, DH).transpose(2, 4, 1, 3, 0).reshape(P, HP * C),
        "wi": L0_ffn_Wi.T,
        "wr": L0_ffn_Wr.transpose(3, 1, 0, 2),
        "ws": L0_ffn_Ws[:, 0].transpose(2, 0, 1),
        "wo2": L0_ffn_Wo.T,
        "route": L0_ffn_route_id.reshape(1, B),
    }
    nc = bacc.Bacc("TRN2", target_bir_lowering=False, num_devices=1)
    feed, args = {}, []
    for name, a in arrays.items():
        a = np.ascontiguousarray(a)
        feed[name] = a
        args.append(nc.dram_tensor(name, a.shape, mybir.dt.from_np(a.dtype), kind="ExternalInput").ap())
    args.append(nc.dram_tensor("out", (P, PAIRS, C), mybir.dt.float32, kind="ExternalOutput").ap())
    build(nc, *args)
    got = run_bass_kernel_spmd(nc, [feed], core_ids=[0]).results[0]["out"]
    got = got.reshape(2, TP, PAIRS // 2, 2, C).transpose(3, 2, 0, 1, 4).reshape(B, TP, C)
    return np.ascontiguousarray(got[:, :T])
```

```python
from contextlib import ExitStack

import numpy as np
import concourse.bass as bass
from concourse import mybir

B, T_IN, C = 64, 125, 64
T, TP = 63, 64
TAPS = 5
NH, DH = 16, 64
HP = NH // 2
HID, NE, NL = 128, 16, 2
P = 128
PAIRS = B // 2
CH = 4
BPC = B // 2 // CH
PPC = PAIRS // CH
XW = 2 * (TP - 1) + TAPS + 1
WSLOT = HID + 1
FP = 4
FB = 2 * FP
FSTEPS = PAIRS // FP
SKEW = 3
PEEL = SKEW + 1
NEG = -1.0e30
LN_EXP_SET = 6
EPS_TOK, EPS_LN, EPS_RMS = 1e-3, 1e-5, 1.1920929e-07

C_ID, C_ONES, C_COS, C_SIN, C_MASK, C_EPS, C_END = 0, 128, 256, 320, 384, 448, 451
V_W, V_B, V_GAMMA, V_BETA, V_ALPHA, V_BI, V_BS, V_BR, V_END = 0, 5, 6, 7, 8, 9, 10, 12, 44
R_QW, R_KW, R_BO, R_END = 0, 64, 128, 192


def build(nc, x, consts, cols, rows, wq, wkv, wo, wi, wr, ws, wo2, route, out):
    f32, f32r, bf16, i32 = mybir.dt.float32, mybir.dt.float32r, mybir.dt.bfloat16, mybir.dt.int32
    ALU, ACT, AX = mybir.AluOpType, mybir.ActivationFunctionType, mybir.AxisListType
    ctx = ExitStack()
    with ctx:
        def sb(name, shape, dt=f32):
            return ctx.enter_context(nc.sbuf_tensor(name, shape, dt))

        def sem(name):
            return ctx.enter_context(nc.semaphore(name))

        cst = sb("cst", [P, C_END])
        col = sb("col", [P, V_END])
        row = sb("row", [P, R_END])
        wq_raw = sb("wq_raw", [P, NH * DH])
        wkv_raw = sb("wkv_raw", [P, 2 * DH])
        wq_hi = sb("wq_hi", [P, NH * DH], f32r)
        wq_lo = sb("wq_lo", [P, NH * DH], f32r)
        wkv_hi = sb("wkv_hi", [P, 2 * DH], f32r)
        wkv_lo = sb("wkv_lo", [P, 2 * DH], f32r)
        wo_sb = sb("wo_sb", [P, HP * C])
        wi_sb = sb("wi_sb", [C, HID])
        ws_sb = sb("ws_sb", [P, NL, HID])
        wo2_sb = sb("wo2_sb", [HID, C])
        route_sb = sb("route_sb", [1, B], i32)
        experts = sb("experts", [P, NE, NL, WSLOT])
        ident_bf = sb("ident_bf", [P, P], bf16)
        mask_bf = sb("mask_bf", [P, 8, TP], bf16)
        taps = sb("taps", [P, TAPS, P])
        kw_row = sb("kw_row", [P, DH])
        ident = cst[:, C_ID:C_ID + P]
        ones_blk = cst[:, C_ONES:C_ONES + P]
        cos = cst[:, C_COS:C_COS + DH]
        sin = cst[:, C_SIN:C_SIN + DH]
        eps_tok, eps_ln, eps_rms = (cst[:, C_EPS + i:C_EPS + i + 1] for i in range(3))

        xin = sb("xin", [P, B // 2, XW])
        y = sb("y", [P, B // 2, TP])
        sq = sb("sq", [P, PPC * C])
        h = sb("h", [P, PAIRS, C])
        xh = sb("xh", [P, PAIRS, C])
        xs = sb("xs", [P, PAIRS, P], f32r)
        kc = sb("kc", [P, PPC, DH])
        ks = sb("ks", [P, PPC, DH])
        sqk = sb("sqk", [P, PPC, DH])
        khat = sb("khat", [P, PPC, DH])
        kbd = sb("kbd", [P, PAIRS, 2, P])
        vbd = sb("vbd", [P, PAIRS, 2, P])
        st = sb("st", [P, CH, 8, PPC])

        x_slot = sb("x_slot", [P, P], f32r)
        k_slot = sb("k_slot", [P, 2, P])
        v_slot = sb("v_slot", [P, 2, P])
        qc, qs, qsq, qrot = (xin[:].rearrange("p b t -> p (b t)")[:, i * NH * DH:(i + 1) * NH * DH]
                             .rearrange("p (n d) -> p n d", d=DH) for i in range(4))
        qms = sb("qms", [P, 2, NH])
        qT = sb("qT", [P, HP, P])
        pr = sb("pr", [P, 2, 8, TP])
        prm = sb("prm", [P, 2, 3, 8])
        pT = sb("pT", [P, 2, 4, 2, TP])
        oT = sb("oT", [P, HP, 2, TP])

        w_slot = sb("w_slot", [P, FB, NL, WSLOT])
        f_st = sb("f_st", [P, 4, FP])
        f_sq = sq[:, 0:FP * C]
        f_x = kc[:, 0:FP, :]
        xh_flat, y_flat = xh[:].rearrange("p n c -> p (n c)"), y[:].rearrange("p b t -> p (b t)")
        f_xT = xh_flat[0:C, 0:FP * P]
        f_h = [xh_flat[:, (i + 1) * FP * P:(i + 2) * FP * P] for i in range(3)]
        f_b = y_flat[:, 0:FP * P]
        f_o = sb("f_o", [P, FP, C])

        ps = ctx.enter_context(nc.psum_tensor("ps", [P, 8, 512], f32))

        S = {n: sem(n) for n in (
            "ld_c", "ld_row", "ld_kv", "ld_q", "ld_o", "ld_ex", "ld_sh", "ld_ff", "ld_rt", "zeroed", "taps_ok", "kw_ok", "bf_ok", "ex_w", "ex_b", "vz",
            "conv", "y_raw", "y_sum", "mean", "y_cen", "y_sq", "y_sqs", "var", "y_std", "y_rs", "y_mul", "y_pos", "y_neg", "y_act",
            "tok", "h_ok", "h_sum", "h_cen", "h_sq", "h_sqs", "h_std", "h_rs", "xh_ok",
            "xTp", "xT_ok", "kv", "kcs", "k_sq", "v_ok", "k_rot", "k_sqs", "k_ln", "k_rs", "k_n1", "khat_ok", "kTp", "kT_ok",
            "ld_xs", "ld_ks", "ld_vs", "wq_h", "wq_l", "wkv_h", "wkv_l", "xs_ok", "q", "q_cs", "q_sq", "q_add", "q_sqs", "q_ln", "q_rs", "q_hat", "qTp", "qT_ok",
            "s_ok", "s_max", "s_sub", "s_exp", "s_sum", "s_rec", "s_prob", "pTp", "pT_ok", "o_ok", "oT_ok", "att", "att_ok",
            "ld_ws", "f_sum", "f_cen", "f_sq", "f_sqs", "f_ln", "f_rs", "f_xn", "f_xTp", "f_xT", "f_1p", "f_1",
            "f_lp", "f_lb", "f_l", "f_op", "f_ob", "f_o", "st_out")}
        ld_x = [sem(f"ld_x{j}") for j in range(CH)]
        ld_c = S["ld_c"]

        def need(eng, name, n):
            if not isinstance(n, int) or n > 0:
                eng.wait_ge(S[name], n)

        def value(eng, n):
            return n if isinstance(n, int) else eng.snap(eng.to_reg(n))

        def live(p):
            return not isinstance(p, int) or 0 <= p < PAIRS

        def steps(eng, step):
            for p in range(PEEL):
                step(p)
            with eng.Fori(PEEL, PAIRS) as p:
                step(p)
            for p in range(PAIRS, PAIRS + SKEW):
                step(p)

        block = ctx.enter_context(nc.Block())

        @block.sync
        def _(sp):
            sp.dma_start(cst[:], consts).then_inc(ld_c, 16)
            sp.dma_start(col[:], cols).then_inc(ld_c, 16)
            for j in range(CH):
                if j == 0:
                    sp.wait_ge(S["zeroed"], 1)
                sp.dma_start(xin[:, j * BPC:(j + 1) * BPC, 2:2 + T_IN],
                             x[:, j * BPC:(j + 1) * BPC, :]).then_inc(ld_x[j], 16)
            sp.dma_start(row[:], rows).then_inc(S["ld_row"], 16)
            sp.dma_start(wkv_raw[:], wkv).then_inc(S["ld_kv"], 16)
            sp.dma_start(wq_raw[:], wq).then_inc(S["ld_q"], 16)
            sp.dma_start(wo_sb[:], wo).then_inc(S["ld_o"], 16)
            sp.dma_start(experts[:, :, :, 0:HID], wr).then_inc(S["ld_ex"], 16)
            sp.dma_start(ws_sb[:], ws).then_inc(S["ld_sh"], 16)
            sp.dma_start(wi_sb[:], wi).then_inc(S["ld_ff"], 16)
            sp.dma_start(wo2_sb[:], wo2).then_inc(S["ld_ff"], 16)
            sp.dma_start(route_sb[:], route).then_inc(S["ld_rt"], 16)
            sp.wait_ge(S["xT_ok"], 2 * CH)
            sp.wait_ge(S["xs_ok"], 2 * CH)
            sp.wait_ge(S["v_ok"], 8 * CH)
            sp.wait_ge(S["kT_ok"], 4 * CH)

            def slots(p):
                if live(p):
                    need(sp, "q", 2 * p)
                    sp.dma_start(x_slot[:].bitcast(f32), xs[:, bass.ds(p, 1), :].bitcast(f32)).then_inc(S["ld_xs"], 16)
                if live(p - 1):
                    need(sp, "s_ok", 2 * (p - 1))
                    sp.dma_start(k_slot[:], kbd[:, bass.ds(p - 1, 1), :, :]).then_inc(S["ld_ks"], 16)
                if live(p - 2):
                    need(sp, "o_ok", 2 * (p - 2))
                    sp.dma_start(v_slot[:], vbd[:, bass.ds(p - 2, 1), :, :]).then_inc(S["ld_vs"], 16)

            steps(sp, slots)

            sp.wait_ge(S["ld_rt"], 16)
            sp.wait_ge(S["ex_w"], 2)
            sp.wait_ge(S["ex_b"], 1)

            def ff_slots(s):
                need(sp, "f_lp", 2 * s)
                need(sp, "f_lb", 2 * s)
                for k in range(FB):
                    half, g2 = (k // 2) % 2, k // 4
                    e = sp.value_load(route_sb[0:1, bass.ds(s * FP + (half * (B // 2) + 2 * g2 + k % 2), 1)],
                                      min_val=0, max_val=NE - 1)
                    sp.dma_start(w_slot[:, k, :, :], experts[:, bass.ds(e, 1), :, :]).then_inc(S["ld_ws"], 16)

            ff_slots(0)
            with sp.Fori(1, FSTEPS) as s:
                ff_slots(s)
                sp.wait_ge(S["f_o"], s)
                sp.dma_start(out[:, bass.ds(s * FP - FP, FP), :], f_o[:]).then_inc(S["st_out"], 16)
            sp.wait_ge(S["f_o"], FSTEPS)
            sp.dma_start(out[:, PAIRS - FP:, :], f_o[:]).then_inc(S["st_out"], 16)
            sp.wait_ge(S["st_out"], 16 * FSTEPS)

        @block.gpsimd
        def _(pool):
            nc.gpsimd.memset(xin[:, :, 0:2], 0.0)
            nc.gpsimd.memset(xin[:, :, 2 + T_IN:XW], 0.0).then_inc(S["zeroed"], 1)
            nc.gpsimd.memset(vbd[:], 0.0)
            nc.gpsimd.memset(kbd[:], 0.0).then_inc(S["vz"], 1)
            pool.wait_ge(ld_c, 32)
            pool.wait_ge(S["ld_sh"], 16)
            pool.wait_ge(S["ld_ex"], 16)
            nc.gpsimd.tensor_tensor(ws_sb[:], ws_sb[:], ident.unsqueeze(1).broadcast_to([P, NL, HID]),
                                    ALU.add).then_inc(S["ex_w"], 1)
            nc.gpsimd.tensor_tensor(experts[:, :, :, HID],
                                    col[:, V_BR:V_BR + NL * NE].rearrange("p (l e) -> p e l", l=NL),
                                    col[:, V_BS:V_BS + NL].unsqueeze(1).broadcast_to([P, NE, NL]),
                                    ALU.add).then_inc(S["ex_b"], 1)
            pool.wait_ge(S["ex_w"], 1)
            nc.gpsimd.tensor_tensor(experts[:, :, :, 0:HID], experts[:, :, :, 0:HID],
                                    ws_sb[:].unsqueeze(1).broadcast_to([P, NE, NL, HID]),
                                    ALU.add).then_inc(S["ex_w"], 1)
            for j in range(CH):
                pool.wait_ge(S["kcs"], 2 * (j + 1))
                need(pool, "k_n1", j)
                nc.gpsimd.tensor_tensor(kc[:], kc[:], ks[:], ALU.add).then_inc(S["k_rot"], 1)

            def normalise(p, b):
                pool.wait_ge(S["s_rec"], 2 * p + b + 1)
                nc.gpsimd.tensor_tensor(pr[:, b], pr[:, b], prm[:, b, 2, :].unsqueeze(2).broadcast_to([P, 8, TP]),
                                        ALU.mult).then_inc(S["s_prob"], 1)

            def step(p):
                if live(p - 2):
                    normalise(p - 2, 1)
                if live(p):
                    for i in range(2):
                        hs = slice(i * 8, i * 8 + 8)
                        pool.wait_ge(S["q_cs"], 2 * p + i + 1)
                        nc.gpsimd.tensor_tensor(qc[:, hs], qc[:, hs], qs[:, hs], ALU.add).then_inc(S["q_add"], 1)
                    pool.wait_ge(S["q_add"], 2 * p + 2)
                    pool.wait_ge(S["q_rs"], p + 1)
                    need(pool, "qTp", 2 * p)
                    nc.gpsimd.tensor_tensor(qrot[:], qc[:], qms[:, 1, :].unsqueeze(2).broadcast_to([P, NH, DH]),
                                            ALU.mult).then_inc(S["q_hat"], 1)
                if live(p - 1):
                    normalise(p - 1, 0)

            steps(pool, step)

            def ff(s):
                pool.wait_ge(S["f_ob"], s + 1)
                nc.gpsimd.tensor_tensor(f_o[:], f_o[:], h[:, bass.ds(s * FP, FP), :], ALU.add).then_inc(S["f_o"], 1)

            with pool.Fori(0, FSTEPS) as s:
                ff(s)

        @block.scalar
        def _(act):
            def copy(o, i, name):
                nc.scalar.activation(o, i, ACT.Copy).then_inc(S[name], 1)

            act.add_instruction(mybir.InstLoadActFuncSet(
                name=nc.get_next_instruction_name(), engine=mybir.EngineType.Activation, act_func_set_id=LN_EXP_SET))
            act.wait_ge(ld_c, 32)
            copy(ident_bf[:], ident, "bf_ok")
            copy(mask_bf[:], cst[:, C_MASK:C_MASK + TP].unsqueeze(1).broadcast_to([P, 8, TP]), "bf_ok")
            act.wait_ge(S["ld_kv"], 16)
            copy(wkv_hi[:], wkv_raw[:], "wkv_h")
            act.wait_ge(S["ld_q"], 16)
            copy(wq_hi[:], wq_raw[:], "wq_h")

            for step in range(CH + 3):
                j = step
                if j < CH:
                    act.wait_ge(S["conv"], j + 1)
                    nc.scalar.activation(y[:, j * BPC:(j + 1) * BPC, :],
                                         ps[:, 0, :].rearrange("p (b t) -> p b t", t=TP),
                                         ACT.Identity, bias=col[:, V_B:V_B + 1]).then_inc(S["y_raw"], 1)
                j = step - 1
                if 0 <= j < CH:
                    yj = y[:, j * BPC:(j + 1) * BPC, :]
                    act.wait_ge(S["y_cen"], j + 1)
                    need(act, "y_sqs", j)
                    need(act, "h_sqs", j - 1)
                    nc.scalar.activation(sq[:].rearrange("p (b t) -> p b t", t=TP), yj,
                                         ACT.Square).then_inc(S["y_sq"], 1)
                    act.wait_ge(S["var"], j + 1)
                    nc.scalar.activation(st[:, j, 2], ps[:, 1, BPC:2 * BPC], ACT.Ln,
                                         bias=eps_tok).then_inc(S["y_std"], 1)
                    act.wait_ge(S["y_std"], j + 1)
                    nc.scalar.activation(st[:, j, 3], st[:, j, 2], ACT.Exp, scale=-0.5).then_inc(S["y_rs"], 1)
                    act.wait_ge(S["y_mul"], 2 * (j + 1))
                    nc.scalar.activation(h[:, j * BPC:(j + 1) * BPC, :], yj, ACT.Relu,
                                         bias=col[:, V_BETA:V_BETA + 1]).then_inc(S["y_pos"], 1)
                j = step - 2
                if 0 <= j < CH:
                    hj = h[:, j * PPC:(j + 1) * PPC, :]
                    act.wait_ge(S["tok"], j + 1)
                    copy(hj, ps[:, 2, :].rearrange("p (n c) -> p n c", c=C), "h_ok")
                    act.wait_ge(S["h_cen"], 2 * (j + 1))
                    need(act, "y_sqs", min(j + 2, CH))
                    nc.scalar.activation(sq[:].rearrange("p (n c) -> p n c", c=C),
                                         xh[:, j * PPC:(j + 1) * PPC, :], ACT.Square).then_inc(S["h_sq"], 1)
                    act.wait_ge(S["h_sqs"], j + 1)
                    nc.scalar.activation(st[:, j, 6], st[:, j, 6], ACT.Ln, scale=1.0 / C,
                                         bias=eps_ln).then_inc(S["h_std"], 1)
                    act.wait_ge(S["h_std"], j + 1)
                    nc.scalar.activation(st[:, j, 7], st[:, j, 6], ACT.Exp, scale=-0.5).then_inc(S["h_rs"], 1)
                j = step - 3
                if j >= 0:
                    for r in range(2):
                        act.wait_ge(S["xTp"], 2 * j + r + 1)
                        p0 = j * PPC + 4 * r
                        copy(xs[0:C, p0:p0 + 4, :], ps[0:C, 3 + r, :].rearrange("c (n t) -> c n t", t=P), "xT_ok")
                    for r in range(2):
                        act.wait_ge(S["kv"], 2 * j + r + 1)
                        act.wait_ge(S["kcs"], 2 * j + r + 1)
                        need(act, "k_sqs", j)
                        kv = ps[:, 5 + r, :].rearrange("p (n f) -> p n f", f=2 * DH)
                        nc.scalar.activation(sqk[:, 4 * r:4 * r + 4, :], kv[:, :, 0:DH],
                                             ACT.Square).then_inc(S["k_sq"], 1)
                        act.wait_ge(S["vz"], 1)
                        p0 = j * PPC + 4 * r
                        for b in range(2):
                            for a in range(2):
                                copy(vbd[a * DH:(a + 1) * DH, p0:p0 + 4, b, a * DH:(a + 1) * DH],
                                     kv[b * TP:(b + 1) * TP, :, DH:], "v_ok")
                    act.wait_ge(S["k_sqs"], j + 1)
                    nc.scalar.activation(st[:, j, 0], st[:, j, 4], ACT.Ln, scale=1.0 / DH,
                                         bias=eps_rms).then_inc(S["k_ln"], 1)
                    act.wait_ge(S["k_ln"], j + 1)
                    nc.scalar.activation(st[:, j, 1], st[:, j, 0], ACT.Exp, scale=-0.5).then_inc(S["k_rs"], 1)
                    for r in range(2):
                        act.wait_ge(S["kTp"], 2 * j + r + 1)
                        p0 = j * PPC + 4 * r
                        for a in range(2):
                            copy(kbd[a * DH:(a + 1) * DH, p0:p0 + 4, :, a * TP:(a + 1) * TP],
                                 ps[0:DH, 7, :].rearrange("d (n b t) -> d n b t", b=2, t=TP), "kT_ok")

            def square_q(p, i):
                act.wait_ge(S["q"], 2 * p + i + 1)
                if i == 0:
                    need(act, "q_sqs", p)
                nc.scalar.activation(qsq[:, i * 8:i * 8 + 8, :], ps[:, i, :].rearrange("p (n d) -> p n d", d=DH),
                                     ACT.Square).then_inc(S["q_sq"], 1)

            def copy_q(p, r):
                act.wait_ge(S["qTp"], 2 * p + r + 1)
                if r == 0:
                    need(act, "s_ok", 2 * p)
                copy(qT[:, 4 * r:4 * r + 4, :], ps[:, 2 + r, :].rearrange("p (n t) -> p n t", t=P), "qT_ok")

            def exp(p, b):
                act.wait_ge(S["s_sub"], 2 * p + b + 1)
                nc.scalar.activation(pr[:, b], pr[:, b], ACT.Exp).then_inc(S["s_exp"], 1)

            def copy_p(p, b):
                act.wait_ge(S["pTp"], 2 * p + b + 1)
                need(act, "o_ok", 2 * (p - 1) + b + 1)
                copy(pT[:, b].rearrange("p n b t -> p (n b t)"), ps[:, 6, :], "pT_ok")

            def copy_o(p, b):
                act.wait_ge(S["o_ok"], 2 * p + b + 1)
                if b == 0:
                    need(act, "att", p)
                copy(oT[:, 4 * b:4 * b + 4, :, :], ps[:, 7, :].rearrange("p (b n t) -> p n b t", b=2, n=4), "oT_ok")

            def step(p):
                if live(p - 3):
                    copy_o(p - 3, 1)
                if live(p - 2):
                    exp(p - 2, 1)
                if live(p):
                    square_q(p, 0)
                if live(p - 2):
                    copy_p(p - 2, 0)
                if live(p):
                    square_q(p, 1)
                if live(p - 1):
                    copy_q(p - 1, 0)
                    copy_q(p - 1, 1)
                if live(p - 2):
                    copy_o(p - 2, 0)
                    copy_p(p - 2, 1)
                if live(p):
                    act.wait_ge(S["q_sqs"], p + 1)
                    nc.scalar.activation(qms[:, 1, :], qms[:, 0, :], ACT.Ln, scale=1.0 / DH,
                                         bias=eps_rms).then_inc(S["q_ln"], 1)
                    act.wait_ge(S["q_ln"], p + 1)
                    nc.scalar.activation(qms[:, 1, :], qms[:, 1, :], ACT.Exp, scale=-0.5).then_inc(S["q_rs"], 1)
                if live(p - 1):
                    exp(p - 1, 0)

            steps(act, step)

            def ff(s):
                act.wait_ge(S["f_cen"], 2 * s + 2)
                nc.scalar.activation(f_sq.rearrange("p (n c) -> p n c", c=C), f_x, ACT.Square).then_inc(S["f_sq"], 1)
                act.wait_ge(S["f_sqs"], s + 1)
                nc.scalar.activation(f_st[:, 2, :], f_st[:, 1, :], ACT.Ln, scale=1.0 / C,
                                     bias=eps_ln).then_inc(S["f_ln"], 1)
                act.wait_ge(S["f_ln"], s + 1)
                nc.scalar.activation(f_st[:, 3, :], f_st[:, 2, :], ACT.Exp, scale=-0.5).then_inc(S["f_rs"], 1)
                act.wait_ge(S["f_xTp"], s + 1)
                need(act, "f_1p", s)
                copy(f_xT, ps[0:C, 0, :], "f_xT")
                act.wait_ge(S["f_1p"], s + 1)
                need(act, "f_lp", 2 * s)
                nc.scalar.activation(f_h[0], ps[:, 1, :], ACT.Relu, bias=col[:, V_BI:V_BI + 1]).then_inc(S["f_1"], 1)
                for l in range(NL):
                    act.wait_ge(S["f_lb"], 2 * s + l + 1)
                    nc.scalar.activation(f_h[l + 1], f_b, ACT.Relu).then_inc(S["f_l"], 1)

            with act.Fori(0, FSTEPS) as s:
                ff(s)

        @block.vector
        def _(dve):
            dve.wait_ge(ld_c, 32)
            for k in range(TAPS):
                last = nc.vector.tensor_scalar(taps[:, k, :], ident, col[:, V_W + k:V_W + k + 1], None, ALU.mult)
            last.then_inc(S["taps_ok"], 1)
            dve.wait_ge(S["ld_row"], 16)
            nc.vector.scalar_tensor_tensor(out=kw_row[:], in0=row[:, R_QW:R_QW + DH], scalar=float(DH) ** -0.5,
                                           in1=row[:, R_KW:R_KW + DH], op0=ALU.mult,
                                           op1=ALU.mult).then_inc(S["kw_ok"], 1)

            dve.wait_ge(S["wkv_h"], 1)
            nc.vector.tensor_tensor(wkv_lo[:], wkv_raw[:], wkv_hi[:].bitcast(f32), ALU.subtract).then_inc(S["wkv_l"], 1)
            dve.wait_ge(S["wq_h"], 1)
            nc.vector.tensor_tensor(wq_lo[:], wq_raw[:], wq_hi[:].bitcast(f32), ALU.subtract).then_inc(S["wq_l"], 1)

            def wide(v, n, w):
                return v.unsqueeze(2).broadcast_to([P, n, w])

            for step in range(CH + 3):
                j = step
                if j < CH:
                    dve.wait_ge(S["y_raw"], j + 1)
                    nc.vector.reduce_sum(st[:, j, 0], y[:, j * BPC:(j + 1) * BPC, 0:T], AX.X).then_inc(S["y_sum"], 1)
                j = step - 1
                if 0 <= j < CH:
                    yj = y[:, j * BPC:(j + 1) * BPC, :]
                    dve.wait_ge(S["mean"], j + 1)
                    nc.vector.tensor_tensor(yj, yj, wide(ps[:, 1, 0:BPC], BPC, TP), ALU.subtract).then_inc(S["y_cen"], 1)
                    dve.wait_ge(S["y_sq"], j + 1)
                    nc.vector.reduce_sum(st[:, j, 1], sq[:].rearrange("p (b t) -> p b t", t=TP)[:, :, 0:T],
                                         AX.X).then_inc(S["y_sqs"], 1)
                    dve.wait_ge(S["y_rs"], j + 1)
                    nc.vector.tensor_scalar(st[:, j, 3], st[:, j, 3], col[:, V_GAMMA:V_GAMMA + 1], None,
                                            ALU.mult).then_inc(S["y_mul"], 1)
                    dve.wait_ge(S["y_mul"], 2 * j + 1)
                    nc.vector.tensor_tensor(yj, yj, wide(st[:, j, 3], BPC, TP), ALU.mult).then_inc(S["y_mul"], 1)
                    dve.wait_ge(S["y_pos"], j + 1)
                    nc.vector.tensor_scalar(yj, yj, col[:, V_BETA:V_BETA + 1], 0.0, ALU.add,
                                            ALU.min).then_inc(S["y_neg"], 1)
                    dve.wait_ge(S["y_neg"], j + 1)
                    nc.vector.scalar_tensor_tensor(out=yj, in0=yj, scalar=col[:, V_ALPHA:V_ALPHA + 1],
                                                   in1=h[:, j * BPC:(j + 1) * BPC, :], op0=ALU.mult,
                                                   op1=ALU.add).then_inc(S["y_act"], 1)
                j = step - 2
                if 0 <= j < CH:
                    hj, xj = h[:, j * PPC:(j + 1) * PPC, :], xh[:, j * PPC:(j + 1) * PPC, :]
                    dve.wait_ge(S["h_ok"], j + 1)
                    nc.vector.reduce_sum(st[:, j, 4], hj, AX.X).then_inc(S["h_sum"], 1)
                    dve.wait_ge(S["h_sum"], j + 1)
                    nc.vector.tensor_scalar(st[:, j, 5], st[:, j, 4], 1.0 / C, None, ALU.mult).then_inc(S["h_cen"], 1)
                    dve.wait_ge(S["h_cen"], 2 * j + 1)
                    nc.vector.tensor_tensor(xj, hj, wide(st[:, j, 5], PPC, C), ALU.subtract).then_inc(S["h_cen"], 1)
                    dve.wait_ge(S["h_sq"], j + 1)
                    nc.vector.reduce_sum(st[:, j, 6], sq[:].rearrange("p (n c) -> p n c", c=C),
                                         AX.X).then_inc(S["h_sqs"], 1)
                    dve.wait_ge(S["h_rs"], j + 1)
                    nc.vector.tensor_tensor(xj, xj, wide(st[:, j, 7], PPC, C), ALU.mult).then_inc(S["xh_ok"], 1)
                j = step - 3
                if j >= 0:
                    for r in range(2):
                        dve.wait_ge(S["xT_ok"], 2 * j + r + 1)
                        p0 = j * PPC + 4 * r
                        nc.vector.tensor_tensor(xs[C:P, p0:p0 + 4, :],
                                                ps[0:C, 3 + r, :].rearrange("c (n t) -> c n t", t=P),
                                                xs[0:C, p0:p0 + 4, :].bitcast(f32),
                                                ALU.subtract).then_inc(S["xs_ok"], 1)
                    need(dve, "k_n1", j)
                    for r in range(2):
                        dve.wait_ge(S["kv"], 2 * j + r + 1)
                        k4 = ps[:, 5 + r, :].rearrange("p (n f) -> p n f", f=2 * DH)
                        n4 = slice(4 * r, 4 * r + 4)
                        nc.vector.tensor_tensor(kc[:, n4, :], k4[:, :, 0:DH],
                                                cos.unsqueeze(1).broadcast_to([P, 4, DH]), ALU.mult)
                        nc.vector.tensor_tensor(ks[:, n4, 0:32], k4[:, :, 32:64],
                                                sin[:, 0:32].unsqueeze(1).broadcast_to([P, 4, 32]), ALU.mult)
                        nc.vector.tensor_tensor(ks[:, n4, 32:64], k4[:, :, 0:32],
                                                sin[:, 32:64].unsqueeze(1).broadcast_to([P, 4, 32]),
                                                ALU.mult).then_inc(S["kcs"], 1)
                    dve.wait_ge(S["k_sq"], 2 * (j + 1))
                    dve.wait_ge(S["h_cen"], 2 * (j + 1))
                    nc.vector.reduce_sum(st[:, j, 4], sqk[:], AX.X).then_inc(S["k_sqs"], 1)
                    dve.wait_ge(S["k_rs"], j + 1)
                    dve.wait_ge(S["k_rot"], j + 1)
                    need(dve, "kTp", 2 * j)
                    nc.vector.tensor_tensor(khat[:], kc[:], wide(st[:, j, 1], PPC, DH), ALU.mult).then_inc(S["k_n1"], 1)
                    dve.wait_ge(S["k_n1"], j + 1)
                    dve.wait_ge(S["kw_ok"], 1)
                    nc.vector.tensor_tensor(khat[:], khat[:], kw_row[:].unsqueeze(1).broadcast_to([P, PPC, DH]),
                                            ALU.mult).then_inc(S["khat_ok"], 1)

            def rope(p, i):
                dve.wait_ge(S["q_sq"], 2 * p + i + 1)
                if i == 0:
                    need(dve, "q_hat", p)
                hs = slice(8 * i, 8 * i + 8)
                q8 = ps[:, i, :].rearrange("p (n d) -> p n d", d=DH)
                nc.vector.tensor_tensor(qc[:, hs, :], q8, cos.unsqueeze(1).broadcast_to([P, 8, DH]), ALU.mult)
                nc.vector.tensor_tensor(qs[:, hs, 0:32], q8[:, :, 32:64],
                                        sin[:, 0:32].unsqueeze(1).broadcast_to([P, 8, 32]), ALU.mult)
                nc.vector.tensor_tensor(qs[:, hs, 32:64], q8[:, :, 0:32],
                                        sin[:, 32:64].unsqueeze(1).broadcast_to([P, 8, 32]),
                                        ALU.mult).then_inc(S["q_cs"], 1)

            def centre(p, b):
                n = 2 * p + b + 1
                dve.wait_ge(S["s_ok"], n)
                s_ps = ps[:, 4 + b, :].rearrange("p (n s) -> p n s", s=TP)
                nc.vector.reduce_max(prm[:, b, 0, :], s_ps, AX.X).then_inc(S["s_max"], 1)
                dve.wait_ge(S["s_max"], n)
                need(dve, "pTp", n - 2)
                nc.vector.tensor_tensor(pr[:, b], s_ps, wide(prm[:, b, 0, :], 8, TP),
                                        ALU.subtract).then_inc(S["s_sub"], 1)

            def probs_sum(p, b):
                n = 2 * p + b + 1
                dve.wait_ge(S["s_exp"], n)
                nc.vector.reduce_sum(prm[:, b, 1, :], pr[:, b], AX.X).then_inc(S["s_sum"], 1)
                dve.wait_ge(S["s_sum"], n)
                nc.vector.reciprocal(prm[:, b, 2, :], prm[:, b, 1, :]).then_inc(S["s_rec"], 1)

            def step(p):
                if live(p - 3):
                    dve.wait_ge(S["att"], p - 2)
                    hp = h[:, bass.ds(p - 3, 1), :]
                    nc.vector.tensor_tensor(hp, hp, ps[:, 6:7, 0:C], ALU.add).then_inc(S["att_ok"], 1)
                if live(p - 2):
                    probs_sum(p - 2, 1)
                if live(p):
                    rope(p, 0)
                    rope(p, 1)
                    dve.wait_ge(S["q_sq"], 2 * p + 2)
                    nc.vector.reduce_sum(qms[:, 0, :], qsq[:], AX.X).then_inc(S["q_sqs"], 1)
                if live(p - 1):
                    centre(p - 1, 0)
                    centre(p - 1, 1)
                    probs_sum(p - 1, 0)

            steps(dve, step)
            dve.wait_ge(S["att_ok"], PAIRS)

            def ff(s):
                hs = h[:, bass.ds(s * FP, FP), :]
                nc.vector.reduce_sum(f_st[:, 0, :], hs, AX.X).then_inc(S["f_sum"], 1)
                dve.wait_ge(S["f_sum"], s + 1)
                nc.vector.tensor_scalar(f_st[:, 1, :], f_st[:, 0, :], 1.0 / C, None, ALU.mult).then_inc(S["f_cen"], 1)
                dve.wait_ge(S["f_cen"], 2 * s + 1)
                need(dve, "f_xTp", s)
                nc.vector.tensor_tensor(f_x, hs, wide(f_st[:, 1, :], FP, C), ALU.subtract).then_inc(S["f_cen"], 1)
                dve.wait_ge(S["f_cen"], 2 * s + 2)
                dve.wait_ge(S["f_sq"], s + 1)
                nc.vector.reduce_sum(f_st[:, 1, :], f_sq.rearrange("p (n c) -> p n c", c=C), AX.X).then_inc(S["f_sqs"], 1)
                dve.wait_ge(S["f_rs"], s + 1)
                nc.vector.tensor_tensor(f_x, f_x, wide(f_st[:, 3, :], FP, C), ALU.mult).then_inc(S["f_xn"], 1)
                for l in range(NL):
                    dve.wait_ge(S["f_lp"], 2 * s + l + 1)
                    if l == 0:
                        need(dve, "f_l", 2 * s)
                    else:
                        dve.wait_ge(S["f_l"], 2 * s + 1)
                    nc.vector.tensor_tensor(f_b.rearrange("p (b t) -> p b t", t=TP),
                                            ps[:, 2 + l, :].rearrange("p (b t) -> p b t", t=TP),
                                            w_slot[:, :, l, HID:].broadcast_to([P, FB, TP]),
                                            ALU.add).then_inc(S["f_lb"], 1)
                dve.wait_ge(S["f_op"], s + 1)
                need(dve, "st_out", 16 * s)
                nc.vector.tensor_tensor(f_o[:], ps[:, 4, 0:FP * C].rearrange("p (n c) -> p n c", c=C),
                                        row[:, R_BO:R_BO + C].unsqueeze(1).broadcast_to([P, FP, C]),
                                        ALU.add).then_inc(S["f_ob"], 1)

            ff(0)
            with dve.Fori(1, FSTEPS) as s:
                ff(s)

        @block.tensor
        def _(pe):
            mm = nc.tensor.matmul
            pe.wait_ge(S["taps_ok"], 1)
            pe.wait_ge(S["zeroed"], 1)
            for step in range(CH + 3):
                j = step
                if j < CH:
                    pe.wait_ge(ld_x[j], 16)
                    need(pe, "y_raw", j)
                    for k in range(TAPS):
                        last = mm(ps[:, 0, :], taps[:, k, :],
                                  xin[:, j * BPC:(j + 1) * BPC, k:k + 2 * TP - 1:2], start=k == 0, stop=k == TAPS - 1)
                    last.then_inc(S["conv"], 1)
                j = step - 1
                if 0 <= j < CH:
                    pe.wait_ge(S["y_sum"], j + 1)
                    need(pe, "y_std", j)
                    mm(ps[:, 1, 0:BPC], ones_blk, st[:, j, 0], start=True, stop=True).then_inc(S["mean"], 1)
                    pe.wait_ge(S["y_sqs"], j + 1)
                    pe.wait_ge(S["y_cen"], j + 1)
                    mm(ps[:, 1, BPC:2 * BPC], ones_blk, st[:, j, 1], start=True, stop=True).then_inc(S["var"], 1)
                j = step - 2
                if 0 <= j < CH:
                    pe.wait_ge(S["y_act"], j + 1)
                    need(pe, "h_ok", j)
                    for g in range(4):
                        b0 = j * BPC + 2 * g
                        last = nc.tensor.transpose(ps[:, 2, g * P:(g + 1) * P], y[:, b0:b0 + 2, :], ident)
                    last.then_inc(S["tok"], 1)
                j = step - 3
                if j >= 0:
                    pe.wait_ge(S["xh_ok"], j + 1)
                    need(pe, "xs_ok", 2 * j)
                    for r in range(2):
                        for n in range(4):
                            last = nc.tensor.transpose(ps[0:C, 3 + r, n * P:(n + 1) * P], xh[:, j * PPC + 4 * r + n, :], ident)
                        last.then_inc(S["xTp"], 1)
                    pe.wait_ge(S["wkv_l"], 1)
                    need(pe, "v_ok", 8 * j)
                    for r in range(2):
                        pe.wait_ge(S["xs_ok"], 2 * j + r + 1)
                        for n in range(4):
                            kv, x_pair = ps[:, 5 + r, n * P:(n + 1) * P], xs[:, j * PPC + 4 * r + n, :]
                            mm(kv, x_pair, wkv_hi[:], start=True, stop=False)
                            last = mm(kv, x_pair, wkv_lo[:], start=False, stop=True)
                        last.then_inc(S["kv"], 1)
                    pe.wait_ge(S["khat_ok"], j + 1)
                    for r in range(2):
                        need(pe, "kT_ok", 2 * (2 * j + r))
                        for n in range(4):
                            last = nc.tensor.transpose(ps[0:DH, 7, n * P:(n + 1) * P], khat[:, 4 * r + n, :], ident)
                        last.then_inc(S["kTp"], 1)

            pe.wait_ge(S["kT_ok"], 4 * CH)
            pe.wait_ge(S["bf_ok"], 2)
            pe.wait_ge(S["wq_l"], 1)
            pe.wait_ge(S["ld_o"], 16)

            def project(p, i):
                if i == 0:
                    pe.wait_ge(S["ld_xs"], 16 * p + 16)
                need(pe, "q_cs", 2 * (p - 1) + i + 1)
                cols = slice(i * 512, (i + 1) * 512)
                mm(ps[:, i, :], x_slot[:], wq_hi[:, cols], start=True, stop=False)
                mm(ps[:, i, :], x_slot[:], wq_lo[:, cols], start=False, stop=True).then_inc(S["q"], 1)

            def transpose_q(p, r):
                if r == 0:
                    pe.wait_ge(S["q_hat"], p + 1)
                need(pe, "qT_ok", 2 * (p - 1) + r + 1)
                for n in range(4):
                    last = nc.tensor.transpose(ps[:, 2 + r, n * P:(n + 1) * P],
                                               qrot[:, 8 * r + 2 * n:8 * r + 2 * n + 2, :], ident)
                last.then_inc(S["qTp"], 1)

            def scores(p, i):
                if i == 0:
                    pe.wait_ge(S["ld_ks"], 16 * p + 16)
                pe.wait_ge(S["qT_ok"], 2 * p + i + 1)
                need(pe, "s_sub", 2 * (p - 1) + i + 1)
                mm(ps[:, 4 + i, :], ident_bf[:], mask_bf[:], start=True, stop=False)
                for n in range(4):
                    for b in range(2):
                        last = mm(ps[b * TP:(b + 1) * TP, 4 + i, n * P:(n + 1) * P],
                                  qT[:, 4 * i + n, b * TP:(b + 1) * TP], k_slot[:, b, :], start=False, stop=n == 3)
                last.then_inc(S["s_ok"], 1)

            def transpose_p(p, i):
                pe.wait_ge(S["s_prob"], 2 * p + i + 1)
                need(pe, "pT_ok", 2 * p + i)
                if i == 0:
                    need(pe, "att_ok", p)
                for n in range(4):
                    last = nc.tensor.transpose(ps[:, 6, n * P:(n + 1) * P], pr[:, i, 2 * n:2 * n + 2, :], ident)
                last.then_inc(S["pTp"], 1)

            def values(p, i):
                if i == 0:
                    pe.wait_ge(S["ld_vs"], 16 * p + 16)
                pe.wait_ge(S["pT_ok"], 2 * p + i + 1)
                need(pe, "oT_ok", 2 * p + i)
                for b in range(2):
                    last = mm(ps[:, 7, b * 256:(b + 1) * 256], v_slot[:, b, :], pT[:, i, :, b, :], start=True, stop=True)
                last.then_inc(S["o_ok"], 1)

            def output(p):
                pe.wait_ge(S["oT_ok"], 2 * p + 2)
                pe.wait_ge(S["pT_ok"], 2 * p + 2)
                for n in range(HP):
                    last = mm(ps[:, 6, 0:C], oT[:, n, :, :], wo_sb[:, n * C:(n + 1) * C], start=n == 0, stop=n == HP - 1)
                last.then_inc(S["att"], 1)

            def step(p):
                if live(p):
                    project(p, 0)
                if live(p - 3):
                    output(p - 3)
                if live(p - 2):
                    transpose_p(p - 2, 0)
                if live(p):
                    project(p, 1)
                if live(p - 1):
                    transpose_q(p - 1, 0)
                    transpose_q(p - 1, 1)
                if live(p - 2):
                    values(p - 2, 0)
                if live(p - 1):
                    scores(p - 1, 0)
                if live(p - 2):
                    transpose_p(p - 2, 1)
                if live(p - 1):
                    scores(p - 1, 1)
                if live(p - 2):
                    values(p - 2, 1)

            steps(pe, step)

            pe.wait_ge(S["ld_ff"], 32)
            pe.wait_ge(S["att_ok"], PAIRS)

            def ff(s):
                normed = value(pe, s + 1)
                pe.wait_ge(ld_c, 32)
                pe.wait_ge(S["f_xn"], normed)
                for n in range(FP):
                    last = nc.tensor.transpose(ps[0:C, 0, n * P:(n + 1) * P], f_x[:, n, :], ident)
                last.then_inc(S["f_xTp"], 1)
                pe.wait_ge(S["f_xT"], s + 1)
                mm(ps[:, 1, :], wi_sb[:], f_xT, start=True, stop=True).then_inc(S["f_1p"], 1)
                pe.wait_ge(S["ld_ws"], 16 * FB * s + 16 * FB)
                for l in range(NL):
                    if l == 0:
                        pe.wait_ge(S["f_1"], s + 1)
                    else:
                        pe.wait_ge(S["f_l"], 2 * s + 1)
                    for b in range(FB):
                        last = mm(ps[:, 2 + l, b * TP:(b + 1) * TP], w_slot[:, b, l, 0:HID],
                                  f_h[l][:, b * TP:(b + 1) * TP], start=True, stop=True)
                    last.then_inc(S["f_lp"], 1)
                pe.wait_ge(S["f_l"], 2 * s + 2)
                need(pe, "f_ob", s)
                for n in range(FP):
                    last = mm(ps[:, 4, n * C:(n + 1) * C], f_h[2][:, n * P:(n + 1) * P], wo2_sb[:], start=True, stop=True)
                last.then_inc(S["f_op"], 1)

            ff(0)
            with pe.Fori(1, FSTEPS) as s:
                ff(s)


def shape_constants():
    c = np.zeros((P, C_END), np.float32)
    c[:, C_ID:C_ID + P] = np.eye(P, dtype=np.float32)
    c[:, C_ONES:C_ONES + P] = np.kron(np.eye(2), np.ones((C, C))) / (T * C)
    half = DH // 2
    freqs = np.float32(10000.0) ** (np.float32(-2.0) * np.arange(half, dtype=np.float32) / np.float32(DH))
    theta = np.tile(np.arange(TP, dtype=np.float32), 2)[:, None] * freqs[None, :]
    c[:, C_COS:C_COS + DH] = np.tile(np.cos(theta), 2)
    c[:, C_SIN:C_SIN + half] = -np.sin(theta)
    c[:, C_SIN + half:C_SIN + DH] = np.sin(theta)
    t, s = np.tile(np.arange(TP), 2)[:, None], np.arange(TP)[None, :]
    c[:, C_MASK:C_MASK + TP] = np.where(s <= t, 0.0, NEG)
    c[:, C_EPS:C_EPS + 3] = [EPS_TOK, EPS_LN, EPS_RMS]
    return c


def kernel(x, L0_tok_w, L0_tok_b, L0_tok_gamma, L0_tok_beta, L0_tok_alpha, L0_attn_wq, L0_attn_wkv, L0_attn_wo,
           L0_attn_q_norm_w, L0_attn_k_norm_w, L0_ffn_route_id, L0_ffn_Wi, L0_ffn_bi, L0_ffn_Wr, L0_ffn_br,
           L0_ffn_Ws, L0_ffn_bs, L0_ffn_Wo, L0_ffn_bo):
    import concourse.bacc as bacc
    from concourse.bass_utils import run_bass_kernel_spmd

    perm = np.concatenate([np.arange(0, DH, 2), np.arange(1, DH, 2)])
    wide = lambda v: np.broadcast_to(v, (P, v.shape[-1]))
    col = lambda v: np.tile(v, P // v.shape[0])[:, None]
    wq = L0_attn_wq.reshape(NH, DH, C)[:, perm].reshape(NH * DH, C)
    arrays = {
        "x_in": x.reshape(2, B // 2, T_IN, C).transpose(0, 3, 1, 2).reshape(P, B // 2, T_IN),
        "consts": shape_constants(),
        "cols": np.concatenate(
            [col(L0_tok_w[k, 0]) for k in range(TAPS)]
            + [col(v) for v in (L0_tok_b, L0_tok_gamma, L0_tok_beta, L0_tok_alpha, L0_ffn_bi)]
            + [L0_ffn_bs[:, 0].T, L0_ffn_br.reshape(NL * NE, HID).T], axis=1),
        "rows": np.concatenate([wide(L0_attn_q_norm_w[perm]), wide(L0_attn_k_norm_w[perm]), wide(L0_ffn_bo)], axis=1),
        "wq": np.tile(wq.T, (2, 1)),
        "wkv": np.tile(np.concatenate([L0_attn_wkv[:DH][perm], L0_attn_wkv[DH:]]).T, (2, 1)),
        "wo": L0_attn_wo.reshape(C, HP, 2, DH).transpose(2, 3, 1, 0).reshape(P, HP * C),
        "wi": L0_ffn_Wi.T,
        "wr": L0_ffn_Wr.transpose(3, 1, 0, 2),
        "ws": L0_ffn_Ws[:, 0].transpose(2, 0, 1),
        "wo2": L0_ffn_Wo.T,
        "route": L0_ffn_route_id.reshape(1, B),
    }
    nc = bacc.Bacc("TRN2", target_bir_lowering=False, num_devices=1)
    feed, args = {}, []
    for name, a in arrays.items():
        a = np.ascontiguousarray(a)
        feed[name] = a
        args.append(nc.dram_tensor(name, a.shape, mybir.dt.from_np(a.dtype), kind="ExternalInput").ap())
    args.append(nc.dram_tensor("out", (P, PAIRS, C), mybir.dt.float32, kind="ExternalOutput").ap())
    build(nc, *args)
    got = run_bass_kernel_spmd(nc, [feed], core_ids=[0]).results[0]["out"]
    got = got.reshape(2, TP, PAIRS // 2, 2, C).transpose(3, 2, 0, 1, 4).reshape(B, TP, C)
    return np.ascontiguousarray(got[:, :T])
```

```python
from contextlib import ExitStack

import numpy as np
import concourse.bass as bass
from concourse import mybir

B, T_IN, C = 64, 125, 64
T, TP = 63, 64
TAPS = 5
NH, DH = 16, 64
HP = NH // 2
HID, NE, NL = 128, 16, 2
P = 128
PAIRS = B // 2
CH = 4
BPC = B // 2 // CH
PPC = PAIRS // CH
XW = 2 * (TP - 1) + TAPS + 1
SKEW = 5
PEEL = SKEW + 1
CONV_PE = CH - 2
NEG = -1.0e30
LN_EXP_SET = 6
EPS_TOK, EPS_LN, EPS_RMS = 1e-3, 1e-5, 1.1920929e-07

C_ID, C_ONES, C_COS, C_SIN, C_MASK, C_EPS, C_EXP, C_FOLD, C_END = 0, 128, 256, 320, 384, 448, 451, 452, 516
V_W, V_B, V_GAMMA, V_BETA, V_ALPHA, V_BI, V_END = 0, 5, 6, 7, 8, 9, 10
R_QW, R_KW, R_BO, R_END = 0, 64, 128, 192


def build(nc, x, consts, cols, rows, wq, wkv, wo, wi, wr, ws, br, bs, wo2, route, route_wide, out):
    f32, f32r, bf16, i32 = mybir.dt.float32, mybir.dt.float32r, mybir.dt.bfloat16, mybir.dt.int32
    ALU, ACT, AX = mybir.AluOpType, mybir.ActivationFunctionType, mybir.AxisListType
    ctx = ExitStack()
    with ctx:
        def sb(name, shape, dt=f32):
            return ctx.enter_context(nc.sbuf_tensor(name, shape, dt))

        def sem(name):
            return ctx.enter_context(nc.semaphore(name))

        cst = sb("cst", [P, C_END])
        col = sb("col", [P, V_END])
        row = sb("row", [P, R_END])
        wq_raw = sb("wq_raw", [P, NH * DH])
        wkv_raw = sb("wkv_raw", [P, 2 * DH])
        wq_hi = sb("wq_hi", [P, NH * DH], f32r)
        wq_lo = sb("wq_lo", [P, NH * DH], f32r)
        wkv_hi = sb("wkv_hi", [P, 2 * DH], f32r)
        wkv_lo = sb("wkv_lo", [P, 2 * DH], f32r)
        wo_sb = sb("wo_sb", [P, HP * C])
        wi_sb = sb("wi_sb", [C, HID])
        ws_sb = sb("ws_sb", [P, NL, HID])
        wo2_sb = sb("wo2_sb", [HID, C])
        route_sb = sb("route_sb", [1, B], i32)
        experts = sb("experts", [P, NE, NL, HID])
        br_sb = sb("br_sb", [NE, NL, HID])
        bs_sb = sb("bs_sb", [NE, NL, HID])
        route_e = sb("route_e", [NE, B], i32)
        one_hot = sb("one_hot", [NE, B])
        bias = sb("bias", [P, NL, B])
        ident_bf = sb("ident_bf", [P, P], bf16)
        mask_bf = sb("mask_bf", [P, 8, TP], bf16)
        taps = sb("taps", [P, TAPS, P])
        kw_row = sb("kw_row", [P, DH])
        ident = cst[:, C_ID:C_ID + P]
        ones_blk = cst[:, C_ONES:C_ONES + P]
        cos = cst[:, C_COS:C_COS + DH]
        sin = cst[:, C_SIN:C_SIN + DH]
        fold = cst[:, C_FOLD:C_FOLD + C]
        expert_id = cst[0:NE, C_EXP:C_EXP + 1]
        eps_tok, eps_ln, eps_rms = (cst[:, C_EPS + i:C_EPS + i + 1] for i in range(3))

        xin = sb("xin", [P, B // 2, XW])
        y = sb("y", [P, B // 2, TP])
        sq_y = sb("sq_y", [P, BPC, TP])
        sq_h = sb("sq_h", [P, PPC, C])
        h = sb("h", [P, PAIRS, C])
        xh = sb("xh", [P, PAIRS, C])
        xs = sb("xs", [P, PAIRS, P], f32r)
        kc = sb("kc", [P, PPC, DH])
        ks = sb("ks", [P, PPC, DH])
        sqk = sb("sqk", [P, PPC, DH])
        v_tok = sb("v_tok", [P, PPC, DH])
        khat = sb("khat", [P, PPC, DH])
        kbd = sb("kbd", [P, PAIRS, 2, P])
        vbd = sb("vbd", [P, PAIRS, 2, P])
        st = sb("st", [P, CH, 9, PPC])

        x_slot = sb("x_slot", [P, P], f32r)
        k_slot = sb("k_slot", [P, 2, P])
        v_slot = sb("v_slot", [P, 2, P])
        qc, qs, qsq, qrot = (xin[:].rearrange("p b t -> p (b t)")[:, i * NH * DH:(i + 1) * NH * DH]
                             .rearrange("p (n d) -> p n d", d=DH) for i in range(4))
        qms = sb("qms", [P, 2, NH])
        qT = sb("qT", [P, HP, P])
        pr = sb("pr", [P, 2, 8, TP])
        prm = sb("prm", [P, 2, 3, 8])
        pT = sb("pT", [P, 2, 4, 2, TP])
        oT = sb("oT", [P, HP, 2, TP])
        att_halves = sb("att_halves", [P, P])

        w_slot = sb("w_slot", [P, 2, NL, HID])
        w_last = sb("w_last", [P, 2, NL, HID])
        f_st = sb("f_st", [P, 3])
        f_x = sb("f_x", [P, C])
        f_sq = sb("f_sq", [P, C])
        f_xT = sb("f_xT", [C, P])
        f_h = [sb(f"f_h{i}", [HID, P]) for i in range(NL + 1)]

        ps = ctx.enter_context(nc.psum_tensor("ps", [P, 8, 512], f32))

        S = {n: sem(n) for n in (
            "ld_c", "ld_col", "ld_row", "ld_kv", "ld_q", "ld_o", "ld_ex", "ld_sh", "ld_ff", "ld_rt",
            "ld_b", "rt_f", "hot", "b_ok", "bias_p", "bias_ok", "zeroed", "taps_ok", "kw_ok",
            "bf_ok", "ex_w", "vz",
            "conv", "y_tap", "y_conv", "y_conv_late", "y_raw", "y_sum", "mean", "y_cen", "y_sq",
            "y_sqs", "var", "y_std", "y_rs", "y_mul", "y_pos", "y_neg", "y_act",
            "tok", "h_ok", "h_sum", "h_cen", "h_sq", "h_sqs", "h_std", "h_rs", "xh_ok",
            "xTp", "xT_ok", "kv", "kcs", "k_sq", "v_ok", "k_rot", "k_sqs", "k_ln", "k_rs", "k_n1",
            "khat_ok", "kTp", "kT_ok",
            "ld_xs", "ld_ks", "ld_vs", "wq_h", "wq_l", "wkv_h", "wkv_l", "xs_ok", "q", "q_cs",
            "q_sq", "q_add", "q_sqs", "q_ln", "q_rs", "q_hat", "qTp", "qT_ok",
            "s_ok", "s_max", "s_sub", "s_exp", "s_sum", "s_rec", "s_prob", "pTp", "pT_ok", "o_ok",
            "oT_ok", "att_p", "att_h", "att", "att_ok",
            "ld_w", "ld_w_last", "f_sum", "f_cen", "f_sq", "f_sqs", "f_ln", "f_rs", "f_xn", "f_xTp",
            "f_xT", "f_ip", "f_i", "f_l0p", "f_l0", "f_l1p", "f_l1", "f_op", "f_ob", "f_o",
            "st_out",
        )}
        ld_x = [sem(f"ld_x{j}") for j in range(CH)]
        v_put, k_put = ([sem(f"{n}_put{j}") for j in range(CH)] for n in "vk")
        ld_c = S["ld_c"]

        def need(eng, name, n):
            if not isinstance(n, int) or n > 0:
                eng.wait_ge(S[name], n)

        def value(eng, n):
            return n if isinstance(n, int) else eng.snap(eng.to_reg(n))

        def live(p):
            return not isinstance(p, int) or 0 <= p < PAIRS

        def tail(p):
            return isinstance(p, int) and p >= PAIRS

        def early(f):
            return tail(f + 2) and f < PAIRS

        def ffn_bank(f):
            return 0 if early(f) and f % 2 == 0 else 3

        def at(p, n):
            return isinstance(p, int) and p == n

        WAVES = CH + 4
        FIRST = WAVES - 2

        def chunk(j):
            return 0 <= j < CH

        def yc(j):
            return y[:, j * BPC:(j + 1) * BPC, :]

        def hc(t, j):
            return t[:, j * PPC:(j + 1) * PPC, :]

        def steps(eng, step, ahead=0):
            for p in range(WAVES - FIRST + ahead, PEEL):
                step(p)
            with eng.Fori(PEEL, PAIRS) as p:
                step(p)
            for p in range(PAIRS, PAIRS + SKEW):
                step(p)

        def tap(j, k):
            return xin[:, j * BPC:(j + 1) * BPC, k:k + 2 * TP - 1:2], col[:, V_W + k:V_W + k + 1]

        block = ctx.enter_context(nc.Block())

        @block.sync
        def _(sp):
            sp.dma_start(col[:], cols).then_inc(S["ld_col"], 16)
            sp.dma_start(cst[:], consts).then_inc(ld_c, 16)
            for j in range(CH):
                if j == 0:
                    sp.wait_ge(S["zeroed"], 1)
                sp.dma_start(xin[:, j * BPC:(j + 1) * BPC, 2:2 + T_IN],
                             x[:, j * BPC:(j + 1) * BPC, :]).then_inc(ld_x[j], 16)
            sp.dma_start(row[:], rows).then_inc(S["ld_row"], 16)
            sp.dma_start(wkv_raw[:], wkv).then_inc(S["ld_kv"], 16)
            sp.dma_start(wq_raw[:], wq).then_inc(S["ld_q"], 16)
            sp.dma_start(wo_sb[:], wo).then_inc(S["ld_o"], 16)
            sp.dma_start(route_e[:], route_wide).then_inc(S["ld_b"], 16)
            sp.dma_start(br_sb[:], br).then_inc(S["ld_b"], 16)
            sp.dma_start(bs_sb[:], bs).then_inc(S["ld_b"], 16)
            sp.dma_start(experts[:], wr).then_inc(S["ld_ex"], 16)
            sp.dma_start(ws_sb[:], ws).then_inc(S["ld_sh"], 16)
            sp.dma_start(wi_sb[:], wi).then_inc(S["ld_ff"], 16)
            sp.dma_start(wo2_sb[:], wo2).then_inc(S["ld_ff"], 16)
            sp.dma_start(route_sb[:], route).then_inc(S["ld_rt"], 16)
            sp.wait_ge(S["ld_rt"], 16)
            sp.wait_ge(S["vz"], 1)

            def put_v(j):
                sp.wait_ge(S["v_ok"], 2 * (j + 1))
                for b in range(2):
                    for a in range(2):
                        sp.dma_start(vbd[a * TP:(a + 1) * TP, j * PPC:(j + 1) * PPC, b, a * DH:(a + 1) * DH],
                                     v_tok[b * TP:(b + 1) * TP]).then_inc(v_put[j], 16)

            def put_k(j):
                sp.wait_ge(S["kT_ok"], 2 * (j + 1))
                sp.dma_start(kbd[DH:P, j * PPC:(j + 1) * PPC, :, TP:P],
                             kbd[0:DH, j * PPC:(j + 1) * PPC, :, 0:TP]).then_inc(k_put[j], 16)

            def slots(p):
                if at(p, 0):
                    sp.wait_ge(S["xT_ok"], 2)
                    sp.wait_ge(S["xs_ok"], 2)
                if live(p):
                    need(sp, "q", 2 * p)
                    sp.dma_start(x_slot[:].bitcast(f32), xs[:, bass.ds(p, 1), :].bitcast(f32)).then_inc(S["ld_xs"], 16)
                f = p - 4
                if live(f):
                    if at(f, 0):
                        sp.wait_ge(S["ex_w"], 5)
                    e = [sp.value_load(route_sb[0:1, bass.ds(f * 2 + b, 1)], min_val=0, max_val=NE - 1) for b in range(2)]
                    last = at(f, PAIRS - 1)
                    if not last:
                        need(sp, "f_l1p", f)
                    for b in range(2):
                        sp.dma_start((w_last if last else w_slot)[:, b],
                                     experts[:, bass.ds(e[b], 1), :, :]).then_inc(S["ld_w_last" if last else "ld_w"], 16)
                if at(p, 1):
                    sp.wait_ge(v_put[0], 4 * 16)
                    sp.wait_ge(k_put[0], 16)
                if at(p, PEEL - 1):
                    sp.wait_ge(S["xT_ok"], 2 * CH)
                    sp.wait_ge(S["xs_ok"], 2 * CH)
                    for j in range(1, CH):
                        sp.wait_ge(v_put[j], 4 * 16)
                        sp.wait_ge(k_put[j], 16)
                if live(p - 1):
                    need(sp, "s_ok", 2 * (p - 1))
                    sp.dma_start(k_slot[:], kbd[:, bass.ds(p - 1, 1), :, :]).then_inc(S["ld_ks"], 16)
                if live(p - 2):
                    need(sp, "o_ok", 2 * (p - 2))
                    sp.dma_start(v_slot[:], vbd[:, bass.ds(p - 2, 1), :, :]).then_inc(S["ld_vs"], 16)
                if live(p - 5):
                    sp.wait_ge(S["f_o"], p - 4)
                    sp.dma_start(out[:, bass.ds(p - 5, 1), :], h[:, bass.ds(p - 5, 1), :]).then_inc(S["st_out"], 16)

            for w in range(WAVES):
                if w >= FIRST - 1:
                    slots(w - FIRST + 1)
                if chunk(w - 4):
                    put_k(w - 4)
                if chunk(w - 3):
                    put_v(w - 3)
            steps(sp, slots, ahead=1)
            sp.wait_ge(S["st_out"], 16 * PAIRS)

        @block.gpsimd
        def _(pool):
            nc.gpsimd.memset(xin[:, :, 0:2], 0.0)
            nc.gpsimd.memset(xin[:, :, 2 + T_IN:XW], 0.0).then_inc(S["zeroed"], 1)
            nc.gpsimd.memset(vbd[:], 0.0)
            nc.gpsimd.memset(kbd[:], 0.0).then_inc(S["vz"], 1)
            last_chunk = CH - 1
            pool.wait_ge(S["ld_col"], 16)
            pool.wait_ge(ld_x[last_chunk], 16)
            for k in range(TAPS):
                x_k, w_k = tap(last_chunk, k)
                if k == 0:
                    nc.gpsimd.tensor_scalar(yc(last_chunk), x_k, w_k, col[:, V_B:V_B + 1], ALU.mult,
                                            ALU.add).then_inc(S["y_conv_late"], 1)
                else:
                    product = (kc, ks)[k % 2]
                    if k > 2:
                        pool.wait_ge(S["y_conv_late"], k - 1)
                    nc.gpsimd.tensor_scalar(product[:], x_k, w_k, None, ALU.mult).then_inc(S["y_tap"], 1)
                    pool.wait_ge(S["y_tap"], k)
                    pool.wait_ge(S["y_conv_late"], k)
                    nc.gpsimd.tensor_tensor(yc(last_chunk), yc(last_chunk), product[:], ALU.add).then_inc(S["y_conv_late"], 1)
            pool.wait_ge(S["ld_b"], 48)
            nc.gpsimd.tensor_tensor(br_sb[:], br_sb[:], bs_sb[:], ALU.add).then_inc(S["b_ok"], 1)
            pool.wait_ge(S["ld_col"], 16)
            pool.wait_ge(ld_c, 16)
            pool.wait_ge(S["ld_sh"], 16)
            pool.wait_ge(S["ld_ex"], 16)
            nc.gpsimd.tensor_tensor(ws_sb[:], ws_sb[:], ident.unsqueeze(1).broadcast_to([P, NL, HID]),
                                    ALU.add).then_inc(S["ex_w"], 1)

            def add_experts(i):
                pool.wait_ge(S["ex_w"], 1)
                quarter = experts[:, i * NE // 4:(i + 1) * NE // 4]
                nc.gpsimd.tensor_tensor(quarter, quarter, ws_sb[:].unsqueeze(1).broadcast_to([P, NE // 4, NL, HID]),
                                        ALU.add).then_inc(S["ex_w"], 1)

            def h_scale(j):
                pool.wait_ge(S["h_rs"], j + 1)
                nc.gpsimd.tensor_tensor(hc(xh, j), hc(xh, j), st[:, j, 7].unsqueeze(2).broadcast_to([P, PPC, C]),
                                        ALU.mult).then_inc(S["xh_ok"], 1)

            def add_k(j):
                pool.wait_ge(S["kcs"], 2 * (j + 1))
                nc.gpsimd.tensor_tensor(kc[:], kc[:], ks[:], ALU.add).then_inc(S["k_rot"], 1)

            def weigh_k(j):
                pool.wait_ge(S["k_n1"], j + 1)
                pool.wait_ge(S["kw_ok"], 1)
                nc.gpsimd.tensor_tensor(khat[:], khat[:], kw_row[:].unsqueeze(1).broadcast_to([P, PPC, DH]),
                                        ALU.mult).then_inc(S["khat_ok"], 1)

            def normalise(p, b):
                pool.wait_ge(S["s_rec"], 2 * p + b + 1)
                nc.gpsimd.tensor_tensor(pr[:, b], pr[:, b], prm[:, b, 2, :].unsqueeze(2).broadcast_to([P, 8, TP]),
                                        ALU.mult).then_inc(S["s_prob"], 1)

            def add_rope(p, i):
                pool.wait_ge(S["q_cs"], 2 * p + i + 1)
                hs = slice(i * 8, i * 8 + 8)
                nc.gpsimd.tensor_tensor(qc[:, hs], qc[:, hs], qs[:, hs], ALU.add).then_inc(S["q_add"], 1)

            def step(p):
                if live(p - 5):
                    pool.wait_ge(S["f_ob"], p - 4)
                    hp = h[:, bass.ds(p - 5, 1), :]
                    nc.gpsimd.tensor_tensor(hp, hp, row[:, R_BO:R_BO + C].unsqueeze(1), ALU.add).then_inc(S["f_o"], 1)
                if live(p):
                    add_rope(p, 0)
                if live(p - 2):
                    normalise(p - 2, 1)
                if live(p):
                    add_rope(p, 1)
                    pool.wait_ge(S["q_add"], 2 * p + 2)
                    pool.wait_ge(S["q_rs"], p + 1)
                    need(pool, "qTp", 2 * p)
                    nc.gpsimd.tensor_tensor(qrot[:], qc[:], qms[:, 1, :].unsqueeze(2).broadcast_to([P, NH, DH]),
                                            ALU.mult).then_inc(S["q_hat"], 1)
                if live(p - 1):
                    normalise(p - 1, 0)

            for w in range(WAVES):
                if chunk(w - 4):
                    weigh_k(w - 4)
                if chunk(w - 2):
                    h_scale(w - 2)
                if w >= FIRST:
                    step(w - FIRST)
                if chunk(w - 3):
                    add_k(w - 3)
                if 2 <= w < 6:
                    add_experts(w - 2)
            steps(pool, step)

        @block.scalar
        def _(act):
            def copy(o, i, name):
                nc.scalar.activation(o, i, ACT.Copy).then_inc(S[name], 1)

            act.add_instruction(mybir.InstLoadActFuncSet(
                name=nc.get_next_instruction_name(), engine=mybir.EngineType.Activation, act_func_set_id=LN_EXP_SET))
            act.wait_ge(S["ld_col"], 16)
            act.wait_ge(ld_c, 16)
            copy(ident_bf[:], ident, "bf_ok")
            copy(mask_bf[:], cst[:, C_MASK:C_MASK + TP].unsqueeze(1).broadcast_to([P, 8, TP]), "bf_ok")
            def weights_high():
                act.wait_ge(S["ld_kv"], 16)
                copy(wkv_hi[:], wkv_raw[:], "wkv_h")
                act.wait_ge(S["ld_q"], 16)
                copy(wq_hi[:], wq_raw[:], "wq_h")

            def conv_bias(j):
                act.wait_ge(S["conv"], 1)
                nc.scalar.activation(yc(j), ps[:, 6, :].rearrange("p (b t) -> p b t", t=TP),
                                     ACT.Identity, bias=col[:, V_B:V_B + 1]).then_inc(S["y_raw"], 1)

            def y_square(j):
                act.wait_ge(S["y_cen"], j + 1)
                need(act, "y_sqs", j)
                nc.scalar.activation(sq_y[:], yc(j), ACT.Square).then_inc(S["y_sq"], 1)

            def y_rsqrt(j):
                act.wait_ge(S["var"], j + 1)
                nc.scalar.activation(st[:, j, 2], ps[:, 1, BPC:2 * BPC], ACT.Ln, bias=eps_tok).then_inc(S["y_std"], 1)
                act.wait_ge(S["y_std"], j + 1)
                nc.scalar.activation(st[:, j, 3], st[:, j, 2], ACT.Exp, scale=-0.5).then_inc(S["y_rs"], 1)

            def y_relu(j):
                act.wait_ge(S["y_mul"], 2 * (j + 1))
                nc.scalar.activation(h[:, j * BPC:(j + 1) * BPC, :], yc(j), ACT.Relu,
                                     bias=col[:, V_BETA:V_BETA + 1]).then_inc(S["y_pos"], 1)

            def h_copy(j):
                act.wait_ge(S["tok"], j + 1)
                nc.scalar.activation(hc(h, j), ps[:, 2, :].rearrange("p (n c) -> p n c", c=C), ACT.Copy).then_inc(S["h_ok"], 1)

            def h_square(j):
                act.wait_ge(S["h_cen"], j + 1)
                need(act, "h_sqs", j)
                nc.scalar.activation(sq_h[:], hc(xh, j), ACT.Square).then_inc(S["h_sq"], 1)

            def h_rsqrt(j):
                act.wait_ge(S["h_sqs"], j + 1)
                nc.scalar.activation(st[:, j, 6], st[:, j, 6], ACT.Ln, scale=1.0 / C, bias=eps_ln).then_inc(S["h_std"], 1)
                act.wait_ge(S["h_std"], j + 1)
                nc.scalar.activation(st[:, j, 7], st[:, j, 6], ACT.Exp, scale=-0.5).then_inc(S["h_rs"], 1)

            def x_copy(j, r):
                act.wait_ge(S["xTp"], j + 1)
                copy(xs[0:C, j * PPC + r:(j + 1) * PPC:2, :],
                     ps[r * C:(r + 1) * C, 3, :].rearrange("c (n t) -> c n t", t=P), "xT_ok")

            def k_square_v_copy(j, r):
                act.wait_ge(S["kv"], 2 * j + r + 1)
                act.wait_ge(S["kcs"], 2 * j + r + 1)
                need(act, "k_sqs", j)
                kv = ps[:, 5 + r, :].rearrange("p (n f) -> p n f", f=2 * DH)
                nc.scalar.activation(sqk[:, 4 * r:4 * r + 4, :], kv[:, :, 0:DH], ACT.Square).then_inc(S["k_sq"], 1)
                if j:
                    act.wait_ge(v_put[j - 1], 4 * 16)
                copy(v_tok[:, 4 * r:4 * r + 4, :], kv[:, :, DH:], "v_ok")

            def k_rsqrt(j):
                act.wait_ge(S["k_sqs"], j + 1)
                nc.scalar.activation(st[:, j, 8], st[:, j, 5], ACT.Ln, scale=1.0 / DH, bias=eps_rms).then_inc(S["k_ln"], 1)
                act.wait_ge(S["k_ln"], j + 1)
                nc.scalar.activation(st[:, j, 8], st[:, j, 8], ACT.Exp, scale=-0.5).then_inc(S["k_rs"], 1)

            def k_copy(j, r):
                act.wait_ge(S["kTp"], j + 1)
                act.wait_ge(S["vz"], 1)
                copy(kbd[0:DH, j * PPC + r:(j + 1) * PPC:2, :, 0:TP],
                     ps[r * DH:(r + 1) * DH, 7, :].rearrange("d (n b t) -> d n b t", b=2, t=TP), "kT_ok")

            def copy_biases():
                act.wait_ge(S["bias_p"], 1)
                copy(bias[:], ps[:, 1, 2 * BPC:2 * BPC + NL * B].rearrange("p (l b) -> p l b", l=NL), "bias_ok")

            def square_q(p, i):
                act.wait_ge(S["q"], 2 * p + i + 1)
                if i == 0:
                    need(act, "q_sqs", p)
                nc.scalar.activation(qsq[:, i * 8:i * 8 + 8, :], ps[:, i, :].rearrange("p (n d) -> p n d", d=DH),
                                     ACT.Square).then_inc(S["q_sq"], 1)

            def copy_q(p, r):
                act.wait_ge(S["qTp"], 2 * p + r + 1)
                if r == 0:
                    need(act, "s_ok", 2 * p)
                copy(qT[:, 4 * r:4 * r + 4, :], ps[:, 2, :].rearrange("p (n t) -> p n t", t=P), "qT_ok")

            def exp(p, b):
                act.wait_ge(S["s_sub"], 2 * p + b + 1)
                nc.scalar.activation(pr[:, b], pr[:, b], ACT.Exp).then_inc(S["s_exp"], 1)

            def copy_p(p, b):
                act.wait_ge(S["pTp"], 2 * p + b + 1)
                need(act, "o_ok", 2 * (p - 1) + b + 1)
                copy(pT[:, b].rearrange("p n b t -> p (n b t)"), ps[:, 6, :], "pT_ok")

            def copy_o(p, b):
                act.wait_ge(S["o_ok"], 2 * p + b + 1)
                if b == 0:
                    need(act, "att", p)
                copy(oT[:, 4 * b:4 * b + 4, :, :], ps[:, 7, :].rearrange("p (b n t) -> p n b t", b=2, n=4), "oT_ok")

            def rsqrt(o, i, scale, eps, name, n):
                act.wait_ge(S[name + "sqs"], n)
                nc.scalar.activation(o, i, ACT.Ln, scale=scale, bias=eps).then_inc(S[name + "ln"], 1)
                act.wait_ge(S[name + "ln"], n)
                nc.scalar.activation(o, o, ACT.Exp, scale=-0.5).then_inc(S[name + "rs"], 1)

            def copy_f(f):
                act.wait_ge(S["f_xTp"], f + 1)
                need(act, "f_ip", f)
                copy(f_xT[:], ps[0:C, ffn_bank(f), 0:P], "f_xT")

            def relu_layer(f, l):
                act.wait_ge(S[f"f_l{l}p"], f + 1)
                need(act, "f_l1p" if l == 0 else "f_op", f)
                for b in range(2):
                    last = nc.scalar.activation(f_h[l + 1][:, b * TP:(b + 1) * TP], ps[:, ffn_bank(f), b * TP:(b + 1) * TP],
                                                ACT.Relu, bias=bias[:, l, bass.ds(f * 2 + b, 1)])
                last.then_inc(S[f"f_l{l}"], 1)

            def step(p):
                f = p - 4
                if live(p - 3):
                    copy_o(p - 3, 1)
                if live(p):
                    square_q(p, 0)
                if live(p - 1):
                    copy_q(p - 1, 0)
                if live(p - 2) and tail(p):
                    exp(p - 2, 1)
                if live(f) and not early(f):
                    copy_f(f)
                if live(p - 2) and not tail(p):
                    exp(p - 2, 1)
                if live(p - 3):
                    act.wait_ge(S["att_p"], p - 2)
                    need(act, "att", p - 3)
                    copy(att_halves[:], ps[:, 7, P:2 * P], "att_h")
                if live(p):
                    square_q(p, 1)
                if live(p - 1):
                    copy_q(p - 1, 1)
                if live(p - 2):
                    copy_p(p - 2, 0)
                if live(f):
                    act.wait_ge(S["f_ip"], f + 1)
                    need(act, "f_l0p", f)
                    nc.scalar.activation(f_h[0][:], ps[:, ffn_bank(f), 0:P], ACT.Relu, bias=col[:, V_BI:V_BI + 1]).then_inc(S["f_i"], 1)
                if live(f):
                    relu_layer(f, 0)
                if live(p):
                    rsqrt(qms[:, 1, :], qms[:, 0, :], 1.0 / DH, eps_rms, "q_", p + 1)
                if live(p - 2):
                    copy_o(p - 2, 0)
                    copy_p(p - 2, 1)
                if live(p - 3) and tail(p):
                    rsqrt(f_st[:, 2:3], f_st[:, 1:2], 1.0 / C, eps_ln, "f_", p - 2)
                if live(f):
                    relu_layer(f, 1)
                if early(f + 1):
                    copy_f(f + 1)
                if live(p - 1):
                    exp(p - 1, 0)
                if live(p - 3) and not tail(p):
                    rsqrt(f_st[:, 2:3], f_st[:, 1:2], 1.0 / C, eps_ln, "f_", p - 2)

            for w in range(WAVES):
                if chunk(w - 2):
                    h_copy(w - 2)
                if chunk(w - 1):
                    y_square(w - 1)
                if w == CONV_PE:
                    conv_bias(w)
                if chunk(w - 3):
                    x_copy(w - 3, 0)
                if chunk(w - 4):
                    k_rsqrt(w - 4)
                if chunk(w - 3):
                    x_copy(w - 3, 1)
                if chunk(w - 2):
                    h_square(w - 2)
                if chunk(w - 1):
                    y_rsqrt(w - 1)
                if chunk(w - 2):
                    h_rsqrt(w - 2)
                if chunk(w - 1):
                    y_relu(w - 1)
                if w == CH:
                    copy_biases()
                if w >= FIRST:
                    step(w - FIRST)
                if chunk(w - 4):
                    k_copy(w - 4, 0)
                if chunk(w - 3):
                    k_square_v_copy(w - 3, 0)
                if chunk(w - 4):
                    k_copy(w - 4, 1)
                if chunk(w - 3):
                    k_square_v_copy(w - 3, 1)
                if w == 1:
                    weights_high()
            steps(act, step)

        @block.vector
        def _(dve):
            dve.wait_ge(S["ld_col"], 16)
            dve.wait_ge(ld_c, 16)
            for k in range(TAPS):
                last = nc.vector.tensor_scalar(taps[:, k, :], ident, col[:, V_W + k:V_W + k + 1], None, ALU.mult)
            last.then_inc(S["taps_ok"], 1)

            def one_hot_routes():
                dve.wait_ge(S["ld_b"], 48)
                nc.vector.tensor_copy(one_hot[:], route_e[:]).then_inc(S["rt_f"], 1)
                dve.wait_ge(S["rt_f"], 1)
                nc.vector.tensor_scalar(one_hot[:], one_hot[:], expert_id, None, ALU.is_equal).then_inc(S["hot"], 1)

            def weights_low():
                dve.wait_ge(S["wkv_h"], 1)
                nc.vector.tensor_tensor(wkv_lo[:], wkv_raw[:], wkv_hi[:].bitcast(f32), ALU.subtract).then_inc(S["wkv_l"], 1)
                dve.wait_ge(S["wq_h"], 1)
                nc.vector.tensor_tensor(wq_lo[:], wq_raw[:], wq_hi[:].bitcast(f32), ALU.subtract).then_inc(S["wq_l"], 1)

            def row_weights():
                dve.wait_ge(S["ld_row"], 16)
                nc.vector.scalar_tensor_tensor(out=kw_row[:], in0=row[:, R_QW:R_QW + DH], scalar=float(DH) ** -0.5,
                                               in1=row[:, R_KW:R_KW + DH], op0=ALU.mult,
                                               op1=ALU.mult).then_inc(S["kw_ok"], 1)

            def wide(v, n, w):
                return v.unsqueeze(2).broadcast_to([P, n, w])

            def conv_early(j):
                dve.wait_ge(ld_x[j], 16)
                for k in range(TAPS):
                    x_k, w_k = tap(j, k)
                    if k == 0:
                        nc.vector.tensor_scalar(yc(j), x_k, w_k, col[:, V_B:V_B + 1], ALU.mult,
                                                ALU.add).then_inc(S["y_conv"], 1)
                    else:
                        dve.wait_ge(S["y_conv"], TAPS * j + k)
                        nc.vector.scalar_tensor_tensor(out=yc(j), in0=x_k, scalar=w_k, in1=yc(j), op0=ALU.mult,
                                                       op1=ALU.add).then_inc(S["y_conv"], 1)

            def y_sum(j):
                if j < CONV_PE:
                    dve.wait_ge(S["y_conv"], TAPS * (j + 1))
                elif j == CONV_PE:
                    dve.wait_ge(S["y_raw"], 1)
                else:
                    dve.wait_ge(S["y_conv_late"], TAPS)
                nc.vector.reduce_sum(st[:, j, 0], yc(j)[:, :, 0:T], AX.X).then_inc(S["y_sum"], 1)

            def y_centre(j):
                dve.wait_ge(S["mean"], j + 1)
                nc.vector.tensor_tensor(yc(j), yc(j), wide(ps[:, 1, 0:BPC], BPC, TP), ALU.subtract).then_inc(S["y_cen"], 1)

            def y_squares_sum(j):
                dve.wait_ge(S["y_sq"], j + 1)
                nc.vector.reduce_sum(st[:, j, 1], sq_y[:, :, 0:T], AX.X).then_inc(S["y_sqs"], 1)

            def y_scale(j):
                dve.wait_ge(S["y_rs"], j + 1)
                nc.vector.tensor_scalar(st[:, j, 3], st[:, j, 3], col[:, V_GAMMA:V_GAMMA + 1], None,
                                        ALU.mult).then_inc(S["y_mul"], 1)
                dve.wait_ge(S["y_mul"], 2 * j + 1)
                nc.vector.tensor_tensor(yc(j), yc(j), wide(st[:, j, 3], BPC, TP), ALU.mult).then_inc(S["y_mul"], 1)

            def y_prelu(j):
                dve.wait_ge(S["y_mul"], 2 * (j + 1))
                low = xh[:, j * BPC:(j + 1) * BPC, :]
                nc.vector.tensor_scalar(low, yc(j), col[:, V_BETA:V_BETA + 1], 0.0, ALU.add, ALU.min).then_inc(S["y_neg"], 1)
                dve.wait_ge(S["y_neg"], j + 1)
                dve.wait_ge(S["y_pos"], j + 1)
                nc.vector.scalar_tensor_tensor(out=yc(j), in0=low, scalar=col[:, V_ALPHA:V_ALPHA + 1],
                                               in1=h[:, j * BPC:(j + 1) * BPC, :], op0=ALU.mult,
                                               op1=ALU.add).then_inc(S["y_act"], 1)

            def h_centre(j):
                dve.wait_ge(S["h_ok"], j + 1)
                nc.vector.reduce_sum(st[:, j, 4], hc(h, j), AX.X).then_inc(S["h_sum"], 1)
                dve.wait_ge(S["h_sum"], j + 1)
                nc.vector.scalar_tensor_tensor(out=hc(xh, j), in0=wide(st[:, j, 4], PPC, C), scalar=-1.0 / C,
                                               in1=hc(h, j), op0=ALU.mult, op1=ALU.add).then_inc(S["h_cen"], 1)

            def h_squares_sum(j):
                dve.wait_ge(S["h_sq"], j + 1)
                nc.vector.reduce_sum(st[:, j, 6], sq_h[:], AX.X).then_inc(S["h_sqs"], 1)

            def x_low(j, r):
                dve.wait_ge(S["xT_ok"], 2 * j + 2)
                pairs = slice(j * PPC + r, (j + 1) * PPC, 2)
                nc.vector.tensor_tensor(xs[C:P, pairs, :], ps[r * C:(r + 1) * C, 3, :].rearrange("c (n t) -> c n t", t=P),
                                        xs[0:C, pairs, :].bitcast(f32), ALU.subtract).then_inc(S["xs_ok"], 1)

            def k_rope(j, r):
                need(dve, "k_n1", j)
                dve.wait_ge(S["kv"], 2 * j + r + 1)
                k4 = ps[:, 5 + r, :].rearrange("p (n f) -> p n f", f=2 * DH)
                n4 = slice(4 * r, 4 * r + 4)
                nc.vector.tensor_tensor(kc[:, n4, :], k4[:, :, 0:DH],
                                        cos.unsqueeze(1).broadcast_to([P, 4, DH]), ALU.mult)
                nc.vector.tensor_tensor(ks[:, n4, 0:32], k4[:, :, 32:64],
                                        sin[:, 0:32].unsqueeze(1).broadcast_to([P, 4, 32]), ALU.mult)
                nc.vector.tensor_tensor(ks[:, n4, 32:64], k4[:, :, 0:32],
                                        sin[:, 32:64].unsqueeze(1).broadcast_to([P, 4, 32]),
                                        ALU.mult).then_inc(S["kcs"], 1)

            def k_squares_sum(j):
                dve.wait_ge(S["k_sq"], 2 * (j + 1))
                nc.vector.reduce_sum(st[:, j, 5], sqk[:], AX.X).then_inc(S["k_sqs"], 1)

            def k_scale(j):
                dve.wait_ge(S["k_rs"], j + 1)
                dve.wait_ge(S["k_rot"], j + 1)
                need(dve, "kTp", j)
                nc.vector.tensor_tensor(khat[:], kc[:], wide(st[:, j, 8], PPC, DH), ALU.mult).then_inc(S["k_n1"], 1)

            def rope(p, i):
                dve.wait_ge(S["q_sq"], 2 * p + i + 1)
                if i == 0:
                    need(dve, "q_hat", p)
                hs = slice(8 * i, 8 * i + 8)
                q8 = ps[:, i, :].rearrange("p (n d) -> p n d", d=DH)
                nc.vector.tensor_tensor(qc[:, hs, :], q8, cos.unsqueeze(1).broadcast_to([P, 8, DH]), ALU.mult)
                nc.vector.tensor_tensor(qs[:, hs, 0:32], q8[:, :, 32:64],
                                        sin[:, 0:32].unsqueeze(1).broadcast_to([P, 8, 32]), ALU.mult)
                nc.vector.tensor_tensor(qs[:, hs, 32:64], q8[:, :, 0:32],
                                        sin[:, 32:64].unsqueeze(1).broadcast_to([P, 8, 32]),
                                        ALU.mult).then_inc(S["q_cs"], 1)

            def centre(p, b):
                n = 2 * p + b + 1
                dve.wait_ge(S["s_ok"], n)
                s_ps = ps[:, 4 + b, :].rearrange("p (n s) -> p n s", s=TP)
                nc.vector.reduce_max(prm[:, b, 0, :], s_ps, AX.X).then_inc(S["s_max"], 1)
                dve.wait_ge(S["s_max"], n)
                need(dve, "pTp", n - 2)
                nc.vector.tensor_tensor(pr[:, b], s_ps, wide(prm[:, b, 0, :], 8, TP),
                                        ALU.subtract).then_inc(S["s_sub"], 1)

            def probs_sum(p, b):
                n = 2 * p + b + 1
                dve.wait_ge(S["s_exp"], n)
                nc.vector.reduce_sum(prm[:, b, 1, :], pr[:, b], AX.X).then_inc(S["s_sum"], 1)
                dve.wait_ge(S["s_sum"], n)
                nc.vector.reciprocal(prm[:, b, 2, :], prm[:, b, 1, :]).then_inc(S["s_rec"], 1)

            def mean_centre(p):
                hp, written = h[:, bass.ds(p, 1), :], value(dve, p + 1)
                dve.wait_ge(ld_c, 16)
                dve.wait_ge(S["att_ok"], written)
                nc.vector.reduce_sum(f_st[:, 0:1], hp, AX.X).then_inc(S["f_sum"], 1)
                dve.wait_ge(S["f_sum"], p + 1)
                need(dve, "f_xTp", p)
                nc.vector.scalar_tensor_tensor(out=f_x[:].unsqueeze(1), in0=f_st[:, 0:1].unsqueeze(2).broadcast_to([P, 1, C]),
                                               scalar=-1.0 / C, in1=hp, op0=ALU.mult, op1=ALU.add).then_inc(S["f_cen"], 1)
                dve.wait_ge(S["f_cen"], p + 1)
                nc.vector.tensor_tensor(f_sq[:], f_x[:], f_x[:], ALU.mult).then_inc(S["f_sq"], 1)
                dve.wait_ge(S["f_sq"], p + 1)
                nc.vector.reduce_sum(f_st[:, 1:2], f_sq[:], AX.X).then_inc(S["f_sqs"], 1)

            def step(p):
                if live(p):
                    rope(p, 0)
                if live(p - 2):
                    probs_sum(p - 2, 1)
                if live(p):
                    rope(p, 1)
                if live(p - 3):
                    dve.wait_ge(S["att"], p - 2)
                    hp = h[:, bass.ds(p - 3, 1), :]
                    nc.vector.tensor_tensor(hp, hp, ps[:, 7:8, 0:C], ALU.add).then_inc(S["att_ok"], 1)
                if live(p):
                    dve.wait_ge(S["q_sq"], 2 * p + 2)
                    nc.vector.reduce_sum(qms[:, 0, :], qsq[:], AX.X).then_inc(S["q_sqs"], 1)
                if live(p - 1):
                    centre(p - 1, 0)
                if live(p - 3):
                    mean_centre(p - 3)
                if live(p - 1):
                    centre(p - 1, 1)
                if live(p - 3):
                    dve.wait_ge(S["f_rs"], p - 2)
                    nc.vector.tensor_scalar(f_x[:], f_x[:], f_st[:, 2:3], None, ALU.mult).then_inc(S["f_xn"], 1)
                if live(p - 4):
                    dve.wait_ge(S["f_op"], p - 3)
                    hp = h[:, bass.ds(p - 4, 1), :]
                    nc.vector.tensor_tensor(hp, hp, ps[:, ffn_bank(p - 4):ffn_bank(p - 4) + 1, 0:C], ALU.add).then_inc(S["f_ob"], 1)
                if live(p - 1):
                    probs_sum(p - 1, 0)

            for w in range(WAVES):
                if chunk(w - 4):
                    k_squares_sum(w - 4)
                if chunk(w - 1):
                    y_centre(w - 1)
                if chunk(w - 2):
                    h_centre(w - 2)
                if w == 1:
                    y_squares_sum(0)
                if w < CONV_PE:
                    conv_early(w)
                if chunk(w):
                    y_sum(w)
                if chunk(w - 1) and w > 1:
                    y_squares_sum(w - 1)
                if chunk(w - 3):
                    x_low(w - 3, 0)
                if chunk(w - 3):
                    x_low(w - 3, 1)
                if chunk(w - 4):
                    k_scale(w - 4)
                if chunk(w - 2):
                    h_squares_sum(w - 2)
                if chunk(w - 1):
                    y_scale(w - 1)
                if w >= FIRST:
                    step(w - FIRST)
                if chunk(w - 1):
                    y_prelu(w - 1)
                if chunk(w - 3):
                    k_rope(w - 3, 0)
                if chunk(w - 3):
                    k_rope(w - 3, 1)
                if w == 1:
                    row_weights()
                    weights_low()
                    one_hot_routes()
            steps(dve, step)

        @block.tensor
        def _(pe):
            mm = nc.tensor.matmul
            pe.wait_ge(S["taps_ok"], 1)
            pe.wait_ge(S["zeroed"], 1)
            def conv(j):
                pe.wait_ge(ld_x[j], 16)
                for k in range(TAPS):
                    last = mm(ps[:, 6, :], taps[:, k, :],
                              xin[:, j * BPC:(j + 1) * BPC, k:k + 2 * TP - 1:2], start=k == 0, stop=k == TAPS - 1)
                last.then_inc(S["conv"], 1)

            def mean(j):
                pe.wait_ge(S["y_sum"], j + 1)
                need(pe, "y_std", j)
                mm(ps[:, 1, 0:BPC], ones_blk, st[:, j, 0], start=True, stop=True).then_inc(S["mean"], 1)

            def variance(j):
                pe.wait_ge(S["y_sqs"], j + 1)
                pe.wait_ge(S["y_cen"], j + 1)
                mm(ps[:, 1, BPC:2 * BPC], ones_blk, st[:, j, 1], start=True, stop=True).then_inc(S["var"], 1)

            def to_tokens(j):
                pe.wait_ge(S["y_act"], j + 1)
                need(pe, "h_ok", j)
                for g in range(4):
                    b0 = j * BPC + 2 * g
                    last = nc.tensor.transpose(ps[:, 2, g * P:(g + 1) * P], y[:, b0:b0 + 2, :], ident)
                last.then_inc(S["tok"], 1)

            def transpose_x(j):
                pe.wait_ge(S["xh_ok"], j + 1)
                need(pe, "xs_ok", 2 * j)
                for n in range(PPC // 2):
                    n0 = j * PPC + 2 * n
                    last = nc.tensor.transpose(ps[:, 3, n * P:(n + 1) * P], xh[:, n0:n0 + 2, :], ident)
                last.then_inc(S["xTp"], 1)

            def project_kv(j, r):
                if r == 0:
                    pe.wait_ge(S["wkv_l"], 1)
                    need(pe, "v_ok", 2 * j)
                if r == 0:
                    pe.wait_ge(S["xs_ok"], 2 * j + 2)
                for n in range(4):
                    kv, x_pair = ps[:, 5 + r, n * P:(n + 1) * P], xs[:, j * PPC + 4 * r + n, :]
                    mm(kv, x_pair, wkv_hi[:], start=True, stop=False)
                    last = mm(kv, x_pair, wkv_lo[:], start=False, stop=True)
                last.then_inc(S["kv"], 1)

            def transpose_k(j):
                pe.wait_ge(S["khat_ok"], j + 1)
                need(pe, "kT_ok", 2 * j)
                for n in range(PPC // 2):
                    last = nc.tensor.transpose(ps[:, 7, n * P:(n + 1) * P], khat[:, 2 * n:2 * n + 2, :], ident)
                last.then_inc(S["kTp"], 1)

            def batch_biases():
                pe.wait_ge(S["hot"], 1)
                pe.wait_ge(S["b_ok"], 1)
                pe.wait_ge(S["y_rs"], CH)
                for l in range(NL):
                    last = mm(ps[:, 1, 2 * BPC + l * B:2 * BPC + (l + 1) * B], br_sb[:, l, :], one_hot[:],
                              start=True, stop=True)
                last.then_inc(S["bias_p"], 1)

            def project(p, i):
                if i == 0:
                    pe.wait_ge(S["ld_xs"], 16 * p + 16)
                    if at(p, 0):
                        pe.wait_ge(S["wq_l"], 1)
                        pe.wait_ge(S["bias_ok"], 1)
                need(pe, "q_cs", 2 * (p - 1) + i + 1)
                cols = slice(i * 512, (i + 1) * 512)
                mm(ps[:, i, :], x_slot[:], wq_hi[:, cols], start=True, stop=False)
                mm(ps[:, i, :], x_slot[:], wq_lo[:, cols], start=False, stop=True).then_inc(S["q"], 1)

            def transpose_q(p, r):
                if r == 0:
                    pe.wait_ge(S["q_hat"], p + 1)
                need(pe, "qT_ok", 2 * p + r)
                for n in range(4):
                    last = nc.tensor.transpose(ps[:, 2, n * P:(n + 1) * P],
                                               qrot[:, 8 * r + 2 * n:8 * r + 2 * n + 2, :], ident)
                last.then_inc(S["qTp"], 1)

            def scores(p, i):
                if i == 0:
                    pe.wait_ge(S["ld_ks"], 16 * p + 16)
                    if at(p, 0):
                        pe.wait_ge(S["bf_ok"], 2)
                        pe.wait_ge(S["xs_ok"], 2 * CH)
                        pe.wait_ge(S["v_ok"], 2 * CH)
                pe.wait_ge(S["qT_ok"], 2 * p + i + 1)
                need(pe, "s_sub", 2 * (p - 1) + i + 1)
                mm(ps[:, 4 + i, :], ident_bf[:], mask_bf[:], start=True, stop=False)
                for n in range(4):
                    for b in range(2):
                        last = mm(ps[b * TP:(b + 1) * TP, 4 + i, n * P:(n + 1) * P],
                                  qT[:, 4 * i + n, b * TP:(b + 1) * TP], k_slot[:, b, :], start=False, stop=n == 3)
                last.then_inc(S["s_ok"], 1)

            def transpose_p(p, i):
                pe.wait_ge(S["s_prob"], 2 * p + i + 1)
                need(pe, "pT_ok", 2 * p + i)
                for n in range(4):
                    last = nc.tensor.transpose(ps[:, 6, n * P:(n + 1) * P], pr[:, i, 2 * n:2 * n + 2, :], ident)
                last.then_inc(S["pTp"], 1)

            def values(p, i):
                if i == 0:
                    pe.wait_ge(S["ld_vs"], 16 * p + 16)
                    if at(p, 0):
                        pe.wait_ge(S["kT_ok"], 2 * CH)
                pe.wait_ge(S["pT_ok"], 2 * p + i + 1)
                need(pe, "oT_ok", 2 * p + i)
                if i == 0:
                    need(pe, "att_ok", p)
                for b in range(2):
                    last = mm(ps[:, 7, b * 256:(b + 1) * 256], v_slot[:, b, :], pT[:, i, :, b, :], start=True, stop=True)
                last.then_inc(S["o_ok"], 1)

            def output(p):
                heads, before = value(pe, 2 * p + 2), value(pe, p)
                pe.wait_ge(ld_c, 16)
                if at(p, 0):
                    pe.wait_ge(S["ld_o"], 16)
                pe.wait_ge(S["oT_ok"], heads)
                need(pe, "att_ok", before)
                for n in range(HP):
                    a = n % 2
                    last = mm(ps[a * C:(a + 1) * C, 7, P:2 * P], wo_sb[:, n * C:(n + 1) * C], oT[:, n, :, :],
                              start=n == a, stop=n == HP - 2 + a)
                last.then_inc(S["att_p"], 1)

            def output_sum(p):
                pe.wait_ge(S["att_h"], p + 1)
                mm(ps[:, 7, 0:C], att_halves[:], fold, start=True, stop=True).then_inc(S["att"], 1)

            def transpose_f(f):
                freed, normed = value(pe, f - 1 if early(f) else f), value(pe, f + 1)
                pe.wait_ge(ld_c, 16)
                need(pe, "f_ob", freed)
                pe.wait_ge(S["f_xn"], normed)
                if ffn_bank(f) == 0:
                    pe.wait_ge(S["q_cs"], 2 * PAIRS)
                nc.tensor.transpose(ps[0:C, ffn_bank(f), 0:P], f_x[:], ident).then_inc(S["f_xTp"], 1)

            def up(f):
                pe.wait_ge(S["f_xT"], f + 1)
                if at(f, 0):
                    pe.wait_ge(S["ld_ff"], 32)
                mm(ps[:, ffn_bank(f), 0:P], wi_sb[:], f_xT[:], start=True, stop=True).then_inc(S["f_ip"], 1)

            def layer(f, l):
                last_pair = at(f, PAIRS - 1)
                w = w_last if last_pair else w_slot
                if l == 0:
                    pe.wait_ge(S["f_i"], f + 1)
                    if last_pair:
                        pe.wait_ge(S["ld_w_last"], 32)
                    else:
                        pe.wait_ge(S["ld_w"], f * 32 + 32)
                else:
                    pe.wait_ge(S["f_l0"], f + 1)
                for b in range(2):
                    last = mm(ps[:, ffn_bank(f), b * TP:(b + 1) * TP], w[:, b, l, :], f_h[l][:, b * TP:(b + 1) * TP],
                              start=True, stop=True)
                last.then_inc(S[f"f_l{l}p"], 1)

            def down(f):
                pe.wait_ge(S["f_l1"], f + 1)
                mm(ps[:, ffn_bank(f), 0:C], f_h[NL][:], wo2_sb[:], start=True, stop=True).then_inc(S["f_op"], 1)

            def step(p):
                f = p - 4
                if live(p):
                    project(p, 0)
                if live(p - 1):
                    transpose_q(p - 1, 0)
                if live(f) and not early(f):
                    transpose_f(f)
                if live(p - 3):
                    output(p - 3)
                if live(p):
                    project(p, 1)
                if live(p - 1):
                    transpose_q(p - 1, 1)
                if live(p - 2):
                    transpose_p(p - 2, 0)
                if live(f):
                    up(f)
                if live(p - 3):
                    output_sum(p - 3)
                if live(p - 1):
                    scores(p - 1, 0)
                if live(f):
                    layer(f, 0)
                if live(p - 2):
                    values(p - 2, 0)
                    transpose_p(p - 2, 1)
                if live(f):
                    layer(f, 1)
                if live(p - 1):
                    scores(p - 1, 1)
                if live(p - 2):
                    values(p - 2, 1)
                if early(f + 1):
                    transpose_f(f + 1)
                if live(f):
                    down(f)

            for w in range(WAVES):
                if chunk(w - 1):
                    mean(w - 1)
                if chunk(w - 2):
                    to_tokens(w - 2)
                if chunk(w - 3):
                    transpose_x(w - 3)
                if w >= FIRST:
                    step(w - FIRST)
                if chunk(w - 1):
                    variance(w - 1)
                if w == 1:
                    conv(CONV_PE)
                if w == CH:
                    batch_biases()
                if chunk(w - 3):
                    project_kv(w - 3, 0)
                if chunk(w - 4):
                    transpose_k(w - 4)
                if chunk(w - 3):
                    project_kv(w - 3, 1)
            steps(pe, step)


def shape_constants():
    c = np.zeros((P, C_END), np.float32)
    c[:, C_ID:C_ID + P] = np.eye(P, dtype=np.float32)
    c[:, C_ONES:C_ONES + P] = np.kron(np.eye(2), np.ones((C, C))) / (T * C)
    half = DH // 2
    freqs = np.float32(10000.0) ** (np.float32(-2.0) * np.arange(half, dtype=np.float32) / np.float32(DH))
    theta = np.tile(np.arange(TP, dtype=np.float32), 2)[:, None] * freqs[None, :]
    c[:, C_COS:C_COS + DH] = np.tile(np.cos(theta), 2)
    c[:, C_SIN:C_SIN + half] = -np.sin(theta)
    c[:, C_SIN + half:C_SIN + DH] = np.sin(theta)
    t, s = np.tile(np.arange(TP), 2)[:, None], np.arange(TP)[None, :]
    c[:, C_MASK:C_MASK + TP] = np.where(s <= t, 0.0, NEG)
    c[:, C_EPS:C_EPS + 3] = [EPS_TOK, EPS_LN, EPS_RMS]
    c[:, C_EXP] = np.arange(P)
    c[:, C_FOLD:C_FOLD + C] = np.tile(np.eye(C), (2, 1))
    return c


def kernel(x, L0_tok_w, L0_tok_b, L0_tok_gamma, L0_tok_beta, L0_tok_alpha, L0_attn_wq, L0_attn_wkv, L0_attn_wo,
           L0_attn_q_norm_w, L0_attn_k_norm_w, L0_ffn_route_id, L0_ffn_Wi, L0_ffn_bi, L0_ffn_Wr, L0_ffn_br,
           L0_ffn_Ws, L0_ffn_bs, L0_ffn_Wo, L0_ffn_bo):
    import concourse.bacc as bacc
    from concourse.bass_utils import run_bass_kernel_spmd

    perm = np.concatenate([np.arange(0, DH, 2), np.arange(1, DH, 2)])
    wide = lambda v: np.broadcast_to(v, (P, v.shape[-1]))
    col = lambda v: np.tile(v, P // v.shape[0])[:, None]
    wq = L0_attn_wq.reshape(NH, DH, C)[:, perm].reshape(NH * DH, C)
    route = L0_ffn_route_id.reshape(2, PAIRS // 2, 2).transpose(1, 0, 2).reshape(B)
    arrays = {
        "x_in": x.reshape(2, B // 2, T_IN, C).transpose(0, 3, 1, 2).reshape(P, B // 2, T_IN),
        "consts": shape_constants(),
        "cols": np.concatenate(
            [col(L0_tok_w[k, 0]) for k in range(TAPS)]
            + [col(v) for v in (L0_tok_b, L0_tok_gamma, L0_tok_beta, L0_tok_alpha, L0_ffn_bi)], axis=1),
        "rows": np.concatenate([wide(L0_attn_q_norm_w[perm]), wide(L0_attn_k_norm_w[perm]), wide(L0_ffn_bo)], axis=1),
        "wq": np.tile(wq.T, (2, 1)),
        "wkv": np.tile(np.concatenate([L0_attn_wkv[:DH][perm], L0_attn_wkv[DH:]]).T, (2, 1)),
        "wo": L0_attn_wo.reshape(C, HP, 2, DH).transpose(2, 3, 1, 0).reshape(P, HP * C),
        "wi": L0_ffn_Wi.T,
        "wr": L0_ffn_Wr.transpose(3, 1, 0, 2),
        "ws": L0_ffn_Ws[:, 0].transpose(2, 0, 1),
        "br": L0_ffn_br.transpose(1, 0, 2),
        "bs": np.broadcast_to(L0_ffn_bs[:, 0], (NE, NL, HID)),
        "wo2": L0_ffn_Wo.T,
        "route": route[None],
        "route_wide": np.broadcast_to(route, (NE, B)),
    }
    nc = bacc.Bacc("TRN2", target_bir_lowering=False, num_devices=1)
    feed, args = {}, []
    for name, a in arrays.items():
        a = np.ascontiguousarray(a)
        feed[name] = a
        args.append(nc.dram_tensor(name, a.shape, mybir.dt.from_np(a.dtype), kind="ExternalInput").ap())
    args.append(nc.dram_tensor("out", (P, PAIRS, C), mybir.dt.float32, kind="ExternalOutput").ap())
    build(nc, *args)
    got = run_bass_kernel_spmd(nc, [feed], core_ids=[0]).results[0]["out"]
    got = got.reshape(2, TP, PAIRS // 2, 2, C).transpose(3, 2, 0, 1, 4).reshape(B, TP, C)
    return np.ascontiguousarray(got[:, :T])
```
